# Optimizing a Trainium2 kernel written in Bass

```python
import numpy as np
import jax
import jax.numpy as jnp

def _softmax(x, axis=-1):
    return jax.nn.softmax(x, axis=axis)

def _gelu(x):
    return jax.nn.gelu(x, approximate=True)

def _silu(x):
    return jax.nn.silu(x)

def _sigmoid(x):
    return jax.nn.sigmoid(x)

def _layernorm(x, axis=-1, eps=1e-05):
    m = jnp.mean(x, axis=axis, keepdims=True)
    v = jnp.var(x, axis=axis, keepdims=True)
    return (x - m) / jnp.sqrt(v + eps)

def _scatter_add(tgt, idx, src, axis=0):
    return tgt.at[idx].add(src)

def _segment_sum(src, seg, n):
    return jax.ops.segment_sum(src, seg, n)
kernel_name = 'mk_xattn_ffn_d1_seqx_r4_9c4b88'

def setup_inputs(seed: int=0):
    np.random.seed(seed)
    _w = jnp.asarray

    def _rec_inputs():
        import jax
        import jax.numpy as jnp
        _rk = jax.random.key(seed)
        x = -0.0002928 + 1 * jax.random.normal(jax.random.fold_in(_rk, 1), (2, 1024, 256), jnp.float32)
        _lenS = 1024 - jax.random.randint(jax.random.fold_in(_rk, 7), (2,), 0, max(1, 1024 // 4) + 1, jnp.int32)
        _lenS2 = 77 - jax.random.randint(jax.random.fold_in(_rk, 8), (2,), 0, max(1, 77 // 4) + 1, jnp.int32)
        _ctx_1024P = jax.random.normal(jax.random.fold_in(_rk, 11), (2, 16, 256), jnp.float32)
        _ctx_1024c = jax.random.dirichlet(jax.random.fold_in(_rk, 511), 0.3 * jnp.ones((16,), jnp.float32), (2, 77))
        _ctx_1024t = jnp.einsum('bsk,bkd->bsd', _ctx_1024c, _ctx_1024P)
        _ctx_1024t = _ctx_1024t * jax.lax.rsqrt(jnp.mean(jnp.square(_ctx_1024t)) + 1e-12) * 0.953939
        ctx_1024 = -0.000514642 + 1.00011 * (_ctx_1024t + 0.3 * jax.random.normal(jax.random.fold_in(_rk, 611), (2, 77, 256), jnp.float32))
        return (x, ctx_1024)
    x, ctx_1024 = _rec_inputs()

    def _L0_xattn_setup():
        import jax, jax.numpy as jnp
        import numpy as np
        EPS = 1e-06
        ROPE_THETA = 10000.0

        def _layernorm(x, w, b):
            mu = jnp.mean(x, axis=-1, keepdims=True)
            var = jnp.var(x, axis=-1, keepdims=True)
            return (x - mu) * jax.lax.rsqrt(var + EPS) * w + b

        def _apply_rope(q):
            b, h, s, d = q.shape
            inv_freq = 1.0 / ROPE_THETA ** (jnp.arange(0, d, 2, dtype=jnp.float32) / d)
            ang = jnp.arange(s, dtype=jnp.float32)[:, None] * inv_freq[None, :]
            cos = jnp.cos(ang)[None, None]
            sin = jnp.sin(ang)[None, None]
            qp = q.reshape(b, h, s, d // 2, 2)
            qe, qo = (qp[..., 0], qp[..., 1])
            out = jnp.stack([qe * cos - qo * sin, qe * sin + qo * cos], axis=-1)
            return out.reshape(b, h, s, d)
        key = jax.random.key(seed)
        ks = jax.random.split(key, 8)
        b, s1, s2, qdim, kdim, H = (2, 512, 256, 256, 256, 16)
        hd = qdim // H
        sc = 0.02
        return {'x': jax.random.normal(ks[0], (b, s1, qdim), jnp.float32), 'y': jax.random.normal(ks[1], (b, s2, kdim), jnp.float32), 'q_w': jax.random.normal(ks[2], (qdim, qdim), jnp.float32) * sc, 'q_b': jnp.zeros((qdim,), jnp.float32), 'kv_w': jax.random.normal(ks[3], (2 * qdim, kdim), jnp.float32) * sc, 'kv_b': jnp.zeros((2 * qdim,), jnp.float32), 'qn_w': jnp.ones((hd,), jnp.float32), 'qn_b': jnp.zeros((hd,), jnp.float32), 'kn_w': jnp.ones((hd,), jnp.float32), 'kn_b': jnp.zeros((hd,), jnp.float32), 'out_w': jax.random.normal(ks[4], (qdim, qdim), jnp.float32) * sc, 'out_b': jnp.zeros((qdim,), jnp.float32)}
    _L0_xattn_all = _L0_xattn_setup()
    _L0_xattn_in = {k: v for k, v in _L0_xattn_all.items() if k in ('q_w', 'q_b', 'kv_w', 'kv_b', 'qn_w', 'qn_b', 'kn_w', 'kn_b', 'out_w', 'out_b')}
    del _L0_xattn_all

    def _L0_ffn_setup():
        import jax, jax.numpy as jnp
        import numpy as np
        TOP_K = 2
        key = jax.random.key(seed)
        ks = jax.random.split(key, 6)
        B, S, D, F, E = (2, 512, 256, 1024, 8)
        sd = 1.0 / np.sqrt(D)
        sf = 1.0 / np.sqrt(F)
        return {'x': jax.random.normal(ks[0], (B, S, D), jnp.float32), 'gate_w': jax.random.normal(ks[1], (D, E), jnp.float32) * sd, 'w1': jax.random.normal(ks[2], (E, D, F), jnp.float32) * sd, 'b1': jax.random.normal(ks[3], (E, F), jnp.float32) * 0.01, 'w2': jax.random.normal(ks[4], (E, F, D), jnp.float32) * sf, 'b2': jax.random.normal(ks[5], (E, D), jnp.float32) * 0.01}
    _L0_ffn_all = _L0_ffn_setup()
    _L0_ffn_in = {k: v for k, v in _L0_ffn_all.items() if k in ('gate_w', 'w1', 'b1', 'w2', 'b2')}
    del _L0_ffn_all
    return {'x': x, 'ctx_1024': ctx_1024, 'L0_xattn_q_w': _L0_xattn_in['q_w'], 'L0_xattn_q_b': _L0_xattn_in['q_b'], 'L0_xattn_kv_w': _L0_xattn_in['kv_w'], 'L0_xattn_kv_b': _L0_xattn_in['kv_b'], 'L0_xattn_qn_w': _L0_xattn_in['qn_w'], 'L0_xattn_qn_b': _L0_xattn_in['qn_b'], 'L0_xattn_kn_w': _L0_xattn_in['kn_w'], 'L0_xattn_kn_b': _L0_xattn_in['kn_b'], 'L0_xattn_out_w': _L0_xattn_in['out_w'], 'L0_xattn_out_b': _L0_xattn_in['out_b'], 'L0_ffn_gate_w': _L0_ffn_in['gate_w'], 'L0_ffn_w1': _L0_ffn_in['w1'], 'L0_ffn_b1': _L0_ffn_in['b1'], 'L0_ffn_w2': _L0_ffn_in['w2'], 'L0_ffn_b2': _L0_ffn_in['b2']}

def reference(x, ctx_1024, L0_xattn_q_w, L0_xattn_q_b, L0_xattn_kv_w, L0_xattn_kv_b, L0_xattn_qn_w, L0_xattn_qn_b, L0_xattn_kn_w, L0_xattn_kn_b, L0_xattn_out_w, L0_xattn_out_b, L0_ffn_gate_w, L0_ffn_w1, L0_ffn_b1, L0_ffn_w2, L0_ffn_b2):
    import jax
    import jax.numpy as jnp

    def _L0_xattn_ref(x, y, q_w, q_b, kv_w, kv_b, qn_w, qn_b, kn_w, kn_b, out_w, out_b):
        import jax, jax.numpy as jnp
        import numpy as np
        EPS = 1e-06
        ROPE_THETA = 10000.0

        def _layernorm(x, w, b):
            mu = jnp.mean(x, axis=-1, keepdims=True)
            var = jnp.var(x, axis=-1, keepdims=True)
            return (x - mu) * jax.lax.rsqrt(var + EPS) * w + b

        def _apply_rope(q):
            b, h, s, d = q.shape
            inv_freq = 1.0 / ROPE_THETA ** (jnp.arange(0, d, 2, dtype=jnp.float32) / d)
            ang = jnp.arange(s, dtype=jnp.float32)[:, None] * inv_freq[None, :]
            cos = jnp.cos(ang)[None, None]
            sin = jnp.sin(ang)[None, None]
            qp = q.reshape(b, h, s, d // 2, 2)
            qe, qo = (qp[..., 0], qp[..., 1])
            out = jnp.stack([qe * cos - qo * sin, qe * sin + qo * cos], axis=-1)
            return out.reshape(b, h, s, d)
        b, s1, c = x.shape
        _, s2, _ = y.shape
        H = 16
        hd = c // H
        scale = hd ** (-0.5)
        q = (x @ q_w.T + q_b).reshape(b, s1, H, hd).transpose(0, 2, 1, 3)
        kv = (y @ kv_w.T + kv_b).reshape(b, s2, 2, H, hd).transpose(2, 0, 3, 1, 4)
        k, v = (kv[0], kv[1])
        q = _layernorm(q, qn_w, qn_b)
        k = _layernorm(k, kn_w, kn_b)
        q = _apply_rope(q) * scale
        attn = jnp.einsum('bhqd,bhkd->bhqk', q, k)
        attn = jax.nn.softmax(attn, axis=-1)
        o = jnp.einsum('bhqk,bhkd->bhqd', attn, v)
        o = o.transpose(0, 2, 1, 3).reshape(b, s1, c)
        return o @ out_w.T + out_b

    def _L0_ffn_ref(x, gate_w, w1, b1, w2, b2):
        import jax, jax.numpy as jnp
        import numpy as np
        TOP_K = 2
        B, S, D = x.shape
        T = B * S
        xf = x.reshape(T, D)
        gate_scores = jax.nn.softmax(xf @ gate_w, axis=-1)
        topk_scores, topk_idx = jax.lax.top_k(gate_scores, TOP_K)
        topk_scores = topk_scores / jnp.sum(topk_scores, axis=-1, keepdims=True)
        h = jax.nn.gelu(jnp.einsum('td,edf->etf', xf, w1) + b1[:, None, :], approximate=False)
        y = jnp.einsum('etf,efd->etd', h, w2) + b2[:, None, :]
        tok = jnp.arange(T)
        y_sel = y[topk_idx.T, tok[None, :]]
        out = jnp.einsum('kt,ktd->td', topk_scores.T, y_sel)
        return out.reshape(B, S, D)
    x = x + _L0_xattn_ref(_layernorm(x, axis=-1), ctx_1024, L0_xattn_q_w, L0_xattn_q_b, L0_xattn_kv_w, L0_xattn_kv_b, L0_xattn_qn_w, L0_xattn_qn_b, L0_xattn_kn_w, L0_xattn_kn_b, L0_xattn_out_w, L0_xattn_out_b)
    x = x + _L0_ffn_ref(_layernorm(x, axis=-1), L0_ffn_gate_w, L0_ffn_w1, L0_ffn_b1, L0_ffn_w2, L0_ffn_b2)
    return x

_drawn_inputs = setup_inputs


def setup_inputs(seed=0):
    import zlib

    import numpy as np

    out = dict(_drawn_inputs(seed))
    spreads = {'L0_xattn_q_b': (0.0, 0.318),
     'L0_xattn_kv_b': (0.0, 0.1),
     'L0_xattn_qn_w': (1.0, 0.6),
     'L0_xattn_qn_b': (0.0, 0.548),
     'L0_xattn_kn_w': (1.0, 0.6),
     'L0_xattn_kn_b': (0.0, 0.8),
     'L0_xattn_out_b': (0.0, 0.1)}
    factors = {'L0_ffn_b1': 8.0, 'L0_ffn_b2': 8.0}
    for name, (base, spread) in spreads.items():
        noise = np.random.default_rng([zlib.crc32(name.encode()), seed]).standard_normal(out[name].shape)
        drawn = base * np.exp(spread * noise) if base else spread * noise
        out[name] = jnp.asarray(drawn.astype(out[name].dtype))
    for name, factor in factors.items():
        out[name] = (out[name] * factor).astype(out[name].dtype)
    return out
```

```python
from contextlib import ExitStack

import concourse.bass as bass
from concourse import mybir

F32 = mybir.dt.float32
BF16 = mybir.dt.bfloat16
I32 = mybir.dt.int32
ALU = mybir.AluOpType
ACT = mybir.ActivationFunctionType
AX = mybir.AxisListType

P = 128
BATCH, SEQ, D = 2, 1024, 256
KEYS = 77
HEADS, HD = 16, 16
EXPERTS, FF = 8, 1024
TOKENS = BATCH * SEQ
TILES = TOKENS // P
PAIRS = TILES // 2
PAIRS_B = PAIRS // BATCH
KD = D // P
KF = FF // P
HPC = HEADS // KD
BLOCKS = 2 * TOKENS // P + EXPERTS - 1
SLOTS = (EXPERTS - 1) * TOKENS + BLOCKS * P
ROWS = TOKENS + P
LN_EPS, HEAD_EPS = 1e-5, 1e-6
FRONT_STEPS = 15
TAIL_STEPS = 28
BLOCK_STEPS = 3


class Steps:

    def __init__(self, eng, sem, base=0):
        self.eng, self.sem, self.base, self.n = eng, sem, base, 0

    def __call__(self, ins):
        ins.then_inc(self.sem, 1)
        self.n += 1

    def sync(self):
        self.eng.wait_ge(self.sem, self.base + self.n)


def xattn_moe_kernel(nc, x, ctx_in, wqT, q_b, wkvT, kv_b, qn_w, qn_b, kn_w, kn_b, woT, out_b,
                     gate_w, w1, b1, w2, b2, c_ident, c_identb, c_upper, c_cos, c_sin, c_sel,
                     c_slots, c_tokens, c_expert, c_block, out):
    x_v = x.rearrange("b (t p) d -> p (b t) d", p=P)
    out_rows = out.rearrange("b s d -> (b s) d")
    slot_table = nc.dram_tensor("slot_table", (SLOTS, 2), I32).ap()
    xn2_rows = nc.dram_tensor("xn2_rows", (ROWS, D), F32).ap()
    acc_rows = nc.dram_tensor("acc_rows", (ROWS, D), F32).ap()

    with ExitStack() as ctx:
        def sb(name, shape, dt=F32):
            return ctx.enter_context(nc.sbuf_tensor(name, shape, dt))

        def sem(name):
            return ctx.enter_context(nc.semaphore(name))

        banks = [ctx.enter_context(nc.psum_tensor(f"bank{n}", [P, 512], F32)) for n in range(8)]
        front_bank, tail_bank = banks[0], banks[1]
        max_banks, score_banks, pv_banks = banks[2:4], banks[4:6], banks[6:8]
        h_banks, hT_banks, y_bank, xg_bank = banks[4:6], banks[6:8], banks[2], banks[0]

        ident, identb = sb("ident", [P, P]), sb("identb", [P, P], BF16)
        upper = sb("upper", [P, 2, P], BF16)
        sel = sb("sel", [2 * HEADS, HEADS, KEYS], BF16)
        cosw, sinw, ropeb = (sb(n, [P, TILES, HD]) for n in ("cosw", "sinw", "ropeb"))
        hw = sb("hw", [P, 4, HD])
        hws = sb("hws", [P, 2, HD])
        tokens = sb("tokens", [P, TILES], I32)
        expert = sb("expert", [P, 3, EXPERTS])
        blockid = sb("blockid", [1, BLOCKS])
        wq, wo = sb("wq", [P, KD, D]), sb("wo", [P, KD, D])
        bq, bo = sb("bq", [P, D]), sb("bo", [P, D])
        gw = sb("gw", [P, KD, EXPERTS])
        w1s = sb("w1s", [P, EXPERTS * KD, FF])
        w2s = sb("w2s", [P, EXPERTS * KF, D])
        b1s = sb("b1s", [P, EXPERTS * KF])
        wsum = sb("wsum", [P, 2 * KD * HEADS + 2 * HEADS])

        kzT = [sb(f"kzT{b}", [P, HEADS, KEYS]) for b in range(BATCH)]
        vaug = [sb(f"vaug{b}", [KEYS, HEADS, HD + 1]) for b in range(BATCH)]
        xall = sb("xall", [P, TILES, D])
        probs = sb("probs", [P, HEADS, 2 * P])
        kz = probs[0:KEYS, 0:8, :].rearrange("p h (a n) -> p (h a) n", a=2)
        kc = probs[0:KEYS, 8, :]
        ksq = probs[0:KEYS, 9, :]
        cT = probs[:, 10, 0:KD * KEYS].rearrange("p (k n) -> p k n", k=KD)
        cin = probs[0:KEYS, 11, :]
        krs = sb("krs", [KEYS, HEADS])[:]
        power = sb("power", [P, 1])
        wkv = probs[:, 12:16, :].rearrange("p (k a) n -> p k (a n)", k=KD)
        bst = sb("bst", [P, 2, 2, 8])
        xn = sb("xn", [P, 2, D])
        xnTs = sb("xnTs", [P, 2, KD, P])
        qc = sb("qc", [P, 2, D])
        qs = sb("qs", [P, 2, D])
        bkv = qc[0:KEYS, :, :].rearrange("p a n -> p (a n)")
        qrs = sb("qrs", [P, 2 * HEADS])
        qr = xn
        qTs, qTb = sb("qTs", [P, KD, 2 * P]), sb("qTb", [P, KD, 2 * P])
        mx = sb("mx", [P, 2, HEADS])
        m2 = sb("m2", [P, 2, 2, HEADS], BF16)
        mTs = sb("mTs", [2 * HEADS, 2 * P], BF16)
        rden = sb("rden", [P, 2, HEADS])
        on = sb("on", [P, 2, D])
        oTs = sb("oTs", [P, 2, KD, P])
        xn2 = sb("xn2", [P, 2, D])
        xn2Ts = oTs
        lsub, pg = sb("lsub", [P, 2, EXPERTS]), sb("pg", [P, 2, EXPERTS])
        pg2 = sb("pg2", [P, 2, EXPERTS])
        cand, same = sb("cand", [P, 2, EXPERTS]), sb("same", [P, 2, EXPERTS])
        gs = sb("gs", [P, 4, 2])
        top = sb("top", [P, 2, 2])
        first = sb("first", [P, 2, 2])
        onehot = sb("onehot", [P, 2, 2, EXPERTS])
        mask = sb("mask", [P, 2, EXPERTS], BF16)
        cum = sb("cum", [P, 3, EXPERTS], BF16)
        pos = sb("pos", [P, 2, EXPERTS])
        posk = sb("posk", [P, 2, 2, EXPERTS])
        slots = sb("slots", [P, 2, 2], I32)
        entry = sb("entry", [P, 2, 2, 2], I32)
        nblk, nblki = sb("nblk", [1, 2, EXPERTS]), sb("nblki", [1, 2, EXPERTS], I32)
        ge, gep = (buf[0:1, :, :].rearrange("p a n -> p (a n)")[:, 0:BLOCKS * (EXPERTS - 1)]
                   .rearrange("p (b e) -> p b e", b=BLOCKS) for buf in (qc, qs))
        metaf = sb("metaf", [1, 3, BLOCKS])
        meta = sb("meta", [1, 2, BLOCKS], I32)
        table = sb("table", [P, BLOCKS, 2], I32)
        gidx, sidx = sb("gidx", [P, 1], I32), sb("sidx", [P, 1], I32)
        b2s = probs[:, 0:8, :]
        hTs = probs[:, 8:12, :].rearrange("p a (b n) -> p (a b) n", n=P)
        xg, yb, ys = probs[:, 12, :], probs[:, 13, :], probs[:, 14, :]
        xgTs = probs[:, 15, :].rearrange("p (k n) -> p k n", n=P)
        hs = xall[:, 0:4, :].rearrange("p t d -> p (t d)")
        hbT = xall[:, 4:8, :].rearrange("p t (a n) -> p (t a) n", n=P)

        names = """const_in rope_in wq_in wkv_in wo_in ctx_in0 ctx_in1 x_first x_rest w1_in w2_in b2_in
            paced power_ready kvar_ready krs_ready xvar_ready xrs_ready qvar_ready qrs_ready
            x1var_ready x1rs_ready prep cT_done cTs_ready kv_done kc_ready ksq_done kz_ready kzT_done kzT_ready
            ctx_ready front_steps tail_steps xn_ready xT_done xnTs_ready q_done qc_ready qsq_done
            qr_ready qT_done qTs_ready qTb_ready s_done max_done m2_ready mT_done mTs_ready
            st_done exp_done pv_done o_ready oT_done oTs_ready a_done x1_ready xn2_ready xn2_stored
            acc_stored xn2T_done xn2Ts_ready logits_done lsub_ready gexp_done mask_ready rank_done
            slots_ready padded scattered entries_written cum_ready count_done meta_steps meta_ready
            table_in idx_ready gathered xgT_done xgTs_ready h_done hs_ready hT_done hbT_ready
            gelu_done y_done block_steps y_ready sidx_ready added out_stored""".split()
        s = {n: sem(n) for n in names}

        def settled(eng):
            eng.sem_inc(s["paced"], 1)

        def steps(eng, step):
            step(-1, 0, front=True)
            step(0, 0, front=True, back=True)
            with eng.Fori(1, PAIRS_B) as i:
                step(i, 0, front=True, back=True, tail=True)
            with eng.Fori(PAIRS_B, PAIRS - 1) as i:
                step(i, 1, front=True, back=True, tail=True)
            step(PAIRS - 1, 1, back=True, tail=True)
            step(PAIRS, 1, tail=True)

        block = ctx.enter_context(nc.Block())

        @block.sync
        def _(sp):
            sp.dma_start(cin, ctx_in[0]).then_inc(s["ctx_in0"], 16)
            sp.dma_start(wkv, wkvT.rearrange("(k p) n -> p k n", p=P)).then_inc(s["wkv_in"], 16)
            sp.dma_start(ident[:], c_ident).then_inc(s["const_in"], 16)
            sp.dma_start(bkv, kv_b.partition_broadcast(KEYS)).then_inc(s["const_in"], 16)
            for n, v in enumerate((qn_w, qn_b, kn_w, kn_b)):
                sp.dma_start(hw[:, n, :], v.partition_broadcast(P)).then_inc(s["const_in"], 16)
            sp.dma_start(xall[:, 0:2, :], x_v[:, 0:2, :]).then_inc(s["x_first"], 16)
            sp.dma_start(wq[:], wqT.rearrange("(k p) n -> p k n", p=P)).then_inc(s["wq_in"], 16)
            sp.dma_start(bq[:], q_b.partition_broadcast(P)).then_inc(s["wq_in"], 16)
            sp.dma_start(cosw[:], c_cos.rearrange("(t p) n -> p t n", p=P)).then_inc(s["rope_in"], 16)
            sp.dma_start(sinw[:], c_sin.rearrange("(t p) n -> p t n", p=P)).then_inc(s["rope_in"], 16)
            sp.dma_start(identb[:], c_identb).then_inc(s["wo_in"], 16)
            sp.dma_start(sel[:], c_sel).then_inc(s["wo_in"], 16)
            sp.dma_start(xall[:, 2:TILES, :], x_v[:, 2:TILES, :]).then_inc(s["x_rest"], 16)
            sp.dma_start(wo[:], woT.rearrange("(k p) n -> p k n", p=P)).then_inc(s["wo_in"], 16)
            sp.dma_start(bo[:], out_b.partition_broadcast(P)).then_inc(s["wo_in"], 16)
            sp.dma_start(gw[:], gate_w.rearrange("(k p) n -> p k n", p=P)).then_inc(s["wo_in"], 16)
            sp.dma_start(upper[:], c_upper).then_inc(s["wo_in"], 16)
            sp.dma_start(tokens[:], c_tokens).then_inc(s["wo_in"], 16)
            sp.dma_start(expert[:], c_expert).then_inc(s["wo_in"], 16)
            sp.dma_start(blockid[:], c_block).then_inc(s["wo_in"], 16)
            sp.dma_start(slot_table, c_slots).then_inc(s["padded"], 16)
            sp.wait_ge(s["prep"], 1)
            sp.dma_start(xn2_rows[TOKENS:ROWS, :], on[:, 0, :]).then_inc(s["xn2_stored"], 16)
            sp.dma_start(acc_rows[TOKENS:ROWS, :], on[:, 0, :]).then_inc(s["acc_stored"], 16)
            sp.wait_ge(s["ctx_ready"], 1)
            sp.dma_start(cin, ctx_in[1]).then_inc(s["ctx_in1"], 16)
            sp.dma_start(b1s[:], b1.rearrange("e (j p) -> p (e j)", p=P),
                         allow_slow_non_contiguous=True).then_inc(s["w1_in"], 16)

            def step(i, b, front=False, back=False, tail=False):
                t = i - 1
                if tail:
                    sp.wait_ge(s["x1_ready"], 2 * t + 2)
                    sp.dma_start(
                        acc_rows[0:TOKENS, :].rearrange("(t p) d -> p t d", p=P)[:, bass.ds(2 * t, 2), :],
                        xall[:, bass.ds(2 * t, 2), :]).then_inc(s["acc_stored"], 16)
                    sp.wait_ge(s["xn2_ready"], 2 * t + 2)
                    sp.dma_start(
                        xn2_rows[0:TOKENS, :].rearrange("(t p) d -> p t d", p=P)[:, bass.ds(2 * t, 2), :],
                        xn2[:]).then_inc(s["xn2_stored"], 16)

            steps(sp, step)
            sp.wait_ge(s["pv_done"], 8 * PAIRS)
            sp.dma_start(b2s, b2.partition_broadcast(P)).then_inc(s["b2_in"], 16)

            sp.wait_ge(s["entries_written"], 1 + PAIRS)
            sp.wait_ge(s["meta_ready"], 1)
            with sp.Fori(0, BLOCKS) as n:
                start = sp.value_load(meta[0:1, 1, bass.ds(n, 1)], min_val=0, max_val=SLOTS - P)
                sp.dma_start(table[:, bass.ds(n, 1), :],
                             slot_table[bass.ds(start, P), :].rearrange("p (a c) -> p a c", a=1)
                             ).then_inc(s["table_in"], 16)
                sp.wait_ge(s["table_in"], 16 * n + 16)
                settled(sp)
            sp.wait_ge(s["added"], 16 * BLOCKS)
            sp.dma_start(out_rows.rearrange("(a r) d -> a (r d)", a=P),
                         acc_rows[0:TOKENS, :].rearrange("(a r) d -> a (r d)", a=P)
                         ).then_inc(s["out_stored"], 16)
            sp.wait_ge(s["out_stored"], 16)

        @block.gpsimd
        def _(pool):
            def root(which, n, buf):
                pool.wait_ge(s[which + "var_ready"], n + 1)
                nc.gpsimd.tensor_tensor(buf, buf, power[0:buf.shape[0], :].to_broadcast(buf.shape), ALU.pow
                                        ).then_inc(s[which + "rs_ready"], 1)

            def step(i, b, front=False, back=False, tail=False):
                f, t = i + 1, i - 1
                if front:
                    root("x", f, bst[:, :, 1, 2])
                    root("q", f, qrs[:])
                if tail:
                    root("x1", t, bst[:, :, 1, 2])
                if front:
                    pool.wait_ge(s["qTs_ready"], f + 1)
                    if back:
                        pool.wait_ge(s["st_done"], 8 * f)
                    settled(pool)
                    nc.gpsimd.tensor_copy(qTb[:], qTs[:]).then_inc(s["qTb_ready"], 1)
                if tail:
                    pool.wait_ge(s["slots_ready"], t + 1)
                    settled(pool)
                    for j in range(2):
                        for k in range(2):
                            nc.gpsimd.indirect_dma_start(
                                slot_table, bass.IndirectOffsetOnAxis(ap=slots[:, j, k:k + 1], axis=0),
                                entry[:, j, k, :], None).then_inc(s["scattered"], 16)
                    pool.wait_ge(s["scattered"], 64 * t + 64)
                    pool.sem_inc(s["entries_written"], 1)

            nc.gpsimd.memset(power[:], -0.5).then_inc(s["power_ready"], 1)
            pool.wait_ge(s["power_ready"], 1)
            for b in range(BATCH):
                root("k", b, krs)
            pool.wait_ge(s["padded"], 16)
            pool.sem_inc(s["entries_written"], 1)
            steps(pool, step)

            def gather(n):
                pool.wait_ge(s["table_in"], 16 * n + 16)
                settled(pool)
                nc.gpsimd.tensor_copy(gidx[:], table[:, bass.ds(n, 1), 0]).then_inc(s["idx_ready"], 1)
                pool.wait_ge(s["idx_ready"], n + 1)
                settled(pool)
                nc.gpsimd.indirect_dma_start(
                    xg, None, xn2_rows, bass.IndirectOffsetOnAxis(ap=gidx[:, 0:1], axis=0)
                ).then_inc(s["gathered"], 16)
                pool.wait_ge(s["gathered"], 16 * n + 16)

            def add_back(n):
                pool.wait_ge(s["y_ready"], n + 1)
                settled(pool)
                nc.gpsimd.indirect_dma_start(
                    acc_rows, bass.IndirectOffsetOnAxis(ap=sidx[:, 0:1], axis=0), ys, None,
                    compute_op=ALU.add).then_inc(s["added"], 16)
                pool.wait_ge(s["added"], 16 * n + 16)

            pool.wait_ge(s["xn2_stored"], 16 + 16 * PAIRS)
            pool.wait_ge(s["acc_stored"], 16 + 16 * PAIRS)
            gather(0)
            pool.wait_ge(s["xgT_done"], 1)
            gather(1)
            with pool.Fori(0, BLOCKS - 2) as n:
                pool.wait_ge(s["xgT_done"], n + 2)
                gather(n + 2)
                add_back(n)
            for n in range(BLOCKS - 2, BLOCKS):
                add_back(n)

        @block.scalar
        def _(act):
            w1_v = w1.rearrange("e (k p) f -> p (e k) f", p=P)
            w2_v = w2.rearrange("e (j p) d -> p (e j) d", p=P)

            def context(b):
                act.wait_ge(s["cT_done"], b + 1)
                nc.scalar.copy(cT, front_bank[:, 0:KD * KEYS].rearrange("p (k n) -> p k n", k=KD)
                               ).then_inc(s["cTs_ready"], 1)
                act.wait_ge(s["kc_ready"], b + 1)
                nc.scalar.activation(ksq, kc, ACT.Square).then_inc(s["ksq_done"], 1)
                for n, (lo, hi) in enumerate(((0, 6), (6, 12), (12, HEADS))):
                    act.wait_ge(s["kzT_done"], 3 * b + n + 1)
                    nc.scalar.copy(kzT[b][:, lo:hi, :],
                                   (max_banks + score_banks)[n][:, 0:(hi - lo) * KEYS]
                                   .rearrange("p (h n) -> p h n", n=KEYS)).then_inc(s["kzT_ready"], 1)

            context(0)
            context(1)
            for e in range(EXPERTS):
                act.dma_start(w1s[:, KD * e:KD * e + KD, :], w1_v[:, KD * e:KD * e + KD, :]
                              ).then_inc(s["w1_in"], 16)
                act.dma_start(w2s[:, KF * e:KF * e + KF, :], w2_v[:, KF * e:KF * e + KF, :]
                              ).then_inc(s["w2_in"], 16)

            def exp(i, g):
                act.wait_ge(s["st_done"], 8 * i + g + 1)
                nc.scalar.activation(probs[0:KEYS, 2 * g:2 * g + 2, :],
                                     score_banks[g % 2][0:KEYS, :].rearrange("p (a n) -> p a n", a=2),
                                     ACT.Exp).then_inc(s["exp_done"], 1)

            def bank_to(buf, bank):
                return nc.scalar.copy(buf[:].rearrange("p a b n -> p (a b n)"), bank[:])

            def step(i, b, front=False, back=False, tail=False):
                f, t = i + 1, i - 1
                if tail:
                    act.wait_ge(s["oT_done"], t + 1)
                    bank_to(oTs, tail_bank).then_inc(s["oTs_ready"], 1)
                if back:
                    exp(i, 0)
                if front:
                    act.wait_ge(s["xT_done"], f + 1)
                    bank_to(xnTs, front_bank).then_inc(s["xnTs_ready"], 1)
                if back:
                    exp(i, 1)
                if front:
                    act.wait_ge(s["qc_ready"], f + 1)
                    nc.scalar.activation(qs[:], qc[:], ACT.Square).then_inc(s["qsq_done"], 1)
                if back:
                    for g in (2, 3, 4):
                        exp(i, g)
                if front:
                    act.wait_ge(s["qT_done"], f + 1)
                    nc.scalar.copy(qTs[:].rearrange("p c n -> p (c n)"), front_bank[:]
                                   ).then_inc(s["qTs_ready"], 1)
                if tail:
                    act.wait_ge(s["xn2T_done"], t + 1)
                    bank_to(xn2Ts, tail_bank).then_inc(s["xn2Ts_ready"], 1)
                if back:
                    exp(i, 5)
                if tail:
                    act.wait_ge(s["lsub_ready"], t + 1)
                    nc.scalar.activation(pg[:], lsub[:], ACT.Exp).then_inc(s["gexp_done"], 1)
                if back:
                    exp(i, 6)
                    exp(i, 7)
                if front:
                    act.wait_ge(s["mT_done"], f + 1)
                    nc.scalar.copy(mTs[:], front_bank[0:2 * HEADS, 0:P].bitcast(BF16)
                                   ).then_inc(s["mTs_ready"], 1)

            steps(act, step)

            def h_copy(n):
                for a in range(2):
                    act.wait_ge(s["h_done"], 2 * n + a + 1)
                    nc.scalar.copy(hs[:, 512 * a:512 * a + 512], h_banks[a][:]).then_inc(s["hs_ready"], 1)

            def gelu(n):
                for a in range(2):
                    act.wait_ge(s["hbT_ready"], 2 * n + a + 1)
                    nc.scalar.activation(hTs[:, 4 * a:4 * a + 4, :], hbT[:, 4 * a:4 * a + 4, :],
                                         ACT.Gelu).then_inc(s["gelu_done"], 1)

            h_copy(0)
            with act.Fori(0, BLOCKS - 1) as n:
                gelu(n)
                h_copy(n + 1)
            gelu(BLOCKS - 1)

        @block.tensor
        def _(pe):
            mm = nc.tensor.matmul

            def context(b):
                pe.wait_ge(s[f"ctx_in{b}"], 16)
                if b == 0:
                    pe.wait_ge(s["const_in"], 96)
                else:
                    pe.wait_ge(s["kc_ready"], 1)
                for k in range(KD):
                    last = nc.tensor.transpose(front_bank[:, k * KEYS:(k + 1) * KEYS],
                                               cin[:, k * P:(k + 1) * P], ident[0:KEYS, 0:KEYS])
                last.then_inc(s["cT_done"], 1)
                pe.wait_ge(s["cTs_ready"], b + 1)
                if b == 0:
                    pe.wait_ge(s["prep"], 2)
                for k in range(KD):
                    last = mm(tail_bank[0:KEYS, :], cT[:, k, :], wkv[:, k, :], start=k == 0, stop=k == KD - 1)
                last.then_inc(s["kv_done"], 1)
                pe.wait_ge(s["kz_ready"], b + 1)
                for n, (lo, hi) in enumerate(((0, 6), (6, 12), (12, HEADS))):
                    if b:
                        pe.wait_ge(s["kzT_ready"], n + 1)
                    for h in range(lo, hi):
                        last = nc.tensor.transpose(
                            (max_banks + score_banks)[n][:, (h - lo) * KEYS:(h - lo + 1) * KEYS],
                            kz[:, h, :], ident[0:KEYS, 0:KEYS])
                    last.then_inc(s["kzT_done"], 1)

            context(0)
            context(1)
            pe.wait_ge(s["kzT_ready"], 6)
            pe.wait_ge(s["ctx_ready"], 2)
            pe.wait_ge(s["prep"], 3)
            pe.wait_ge(s["wo_in"], 16 * 9)

            def scores(i, b, g):
                if g == 0:
                    pe.wait_ge(s["qTb_ready"], i + 1)
                    pe.wait_ge(s["mTs_ready"], i + 1)
                if not (isinstance(i, int) and i == 0 and g < 2):
                    pe.wait_ge(s["exp_done"], 8 * i + g - 1)
                for a in range(2):
                    h = 2 * g + a
                    to = score_banks[g % 2][0:KEYS, a * 2 * P:(a + 1) * 2 * P]
                    mm(to, kzT[b][:, h, :], qTb[:, h // HPC, :], start=True, stop=False)
                    last = mm(to, sel[:, h, :], mTs[:], start=False, stop=True)
                last.then_inc(s["st_done"], 1)

            def values(i, b, g):
                pe.wait_ge(s["exp_done"], 8 * i + g + 1)
                if g == 0 and not (isinstance(i, int) and i == 0):
                    pe.wait_ge(s["o_ready"], 2 * i)
                for j in range(2):
                    for h in (2 * g, 2 * g + 1):
                        last = mm(pv_banks[j][:, h * (HD + 1):(h + 1) * (HD + 1)],
                                  probs[0:KEYS, h, j * P:(j + 1) * P], vaug[b][:, h, :],
                                  start=True, stop=True)
                last.then_inc(s["pv_done"], 1)

            def maxima(f, j):
                n = 0
                if j == 0:
                    pe.wait_ge(s["qTs_ready"], f + 1)
                kb = kz_of(f)
                for c in range(KD):
                    for g in range(2):
                        if not (isinstance(f, int) and f == 0 and j == 0 and n < 2):
                            pe.wait_ge(s["max_done"], 8 * f + 4 * j + n - 1)
                        mm(max_banks[n % 2][:, 0:4 * KEYS], qTs[:, c, j * P:(j + 1) * P],
                           kb[:, HPC * c + 4 * g:HPC * c + 4 * g + 4, :].rearrange("p h n -> p (h n)"),
                           start=True, stop=True).then_inc(s["s_done"], 1)
                        n += 1

            front_batch = [0]

            def kz_of(f):
                return kzT[front_batch[0]]

            def transposes(bank, src, split):
                for j in range(2):
                    for k in range(KD):
                        at = (2 * j + k if split else 2 * k + j) * P
                        last = nc.tensor.transpose(bank[:, at:at + P], src[:, j, k * P:(k + 1) * P], ident[:])
                return last

            def project(bank, lhs, w, n):
                for j in range(2):
                    for k in range(KD):
                        last = mm(bank[:, j * n:(j + 1) * n], lhs[:, j, k, :], w[:, k, :],
                                  start=k == 0, stop=k == KD - 1)
                return last

            def step(i, b, front=False, back=False, tail=False):
                f, t = i + 1, i - 1
                if tail:
                    pe.wait_ge(s["o_ready"], 2 * t + 2)
                    transposes(tail_bank, on, True).then_inc(s["oT_done"], 1)
                if back:
                    scores(i, b, 0)
                if front:
                    pe.wait_ge(s["xn_ready"], 2 * f + 2)
                    if back:
                        pe.wait_ge(s["mTs_ready"], f)
                    transposes(front_bank, xn, True).then_inc(s["xT_done"], 1)
                if back:
                    scores(i, b, 1)
                if front:
                    pe.wait_ge(s["xnTs_ready"], f + 1)
                    project(front_bank, xnTs, wq, D).then_inc(s["q_done"], 1)
                if tail:
                    pe.wait_ge(s["oTs_ready"], t + 1)
                    project(tail_bank, oTs, wo, D).then_inc(s["a_done"], 1)
                if back:
                    for g in range(3):
                        scores(i, b, g + 2)
                        values(i, b, g)
                if front:
                    pe.wait_ge(s["qr_ready"], f + 1)
                    transposes(front_bank, qr, False).then_inc(s["qT_done"], 1)
                if tail:
                    pe.wait_ge(s["xn2_ready"], 2 * t + 2)
                    transposes(tail_bank, xn2, True).then_inc(s["xn2T_done"], 1)
                if back:
                    scores(i, b, 5)
                    values(i, b, 3)
                if front:
                    maxima(f, 0)
                if tail:
                    pe.wait_ge(s["xn2Ts_ready"], t + 1)
                    project(tail_bank, xn2Ts, gw, EXPERTS).then_inc(s["logits_done"], 1)
                if back:
                    scores(i, b, 6)
                    values(i, b, 4)
                    scores(i, b, 7)
                    values(i, b, 5)
                if front:
                    maxima(f, 1)
                if tail:
                    pe.wait_ge(s["mask_ready"], t + 1)
                    for j in range(2):
                        to = tail_bank[:, 64 + j * EXPERTS:64 + (j + 1) * EXPERTS]
                        mm(to, upper[:, 0, :], mask[:, j, :], start=True, stop=False)
                        last = mm(to, upper[:, 1, :], cum[:, j, :], start=False, stop=True)
                    last.then_inc(s["rank_done"], 1)
                if back:
                    values(i, b, 6)
                if front:
                    pe.wait_ge(s["m2_ready"], f + 1)
                    for j in range(2):
                        last = nc.tensor.transpose(
                            front_bank[0:2 * HEADS, j * P // 2:(j + 1) * P // 2].bitcast(BF16),
                            m2[:, j, :, :].rearrange("p a h -> p (a h)"), identb[:])
                    last.then_inc(s["mT_done"], 1)
                if back:
                    values(i, b, 7)

            step(-1, 0, front=True)
            step(0, 0, front=True, back=True)
            with pe.Fori(1, PAIRS_B - 1) as i:
                step(i, 0, front=True, back=True, tail=True)
            front_batch[0] = 1
            step(PAIRS_B - 1, 0, front=True, back=True, tail=True)
            with pe.Fori(PAIRS_B, PAIRS - 1) as i:
                step(i, 1, front=True, back=True, tail=True)
            step(PAIRS - 1, 1, back=True, tail=True)
            step(PAIRS, 1, tail=True)
            pe.wait_ge(s["cum_ready"], 1)
            mm(tail_bank[:, 128:128 + EXPERTS], upper[:, 1, :], cum[:, 2, :], start=True, stop=True
               ).then_inc(s["count_done"], 1)

            def xg_turn(n):
                pe.wait_ge(s["gathered"], 16 * n + 16)
                for k in range(KD):
                    last = nc.tensor.transpose(xg_bank[:, k * P:(k + 1) * P], xg[:, k * P:(k + 1) * P], ident[:])
                last.then_inc(s["xgT_done"], 1)

            def up(n):
                e = pe.value_load(meta[0:1, 0, bass.ds(n, 1)], min_val=0, max_val=EXPERTS - 1)
                pe.wait_ge(s["xgTs_ready"], n + 1)
                for a in range(2):
                    for k in range(KD):
                        last = mm(h_banks[a][:], xgTs[:, k, :],
                                  w1s[:, bass.ds(KD * e + k, 1), 512 * a:512 * a + 512].rearrange("p a f -> p (a f)"),
                                  start=k == 0, stop=k == KD - 1)
                    last.then_inc(s["h_done"], 1)

            def h_turn(n):
                for a in range(2):
                    pe.wait_ge(s["hs_ready"], 2 * n + a + 1)
                    for j in range(4):
                        last = nc.tensor.transpose(hT_banks[a][:, j * P:(j + 1) * P],
                                                   hs[:, (4 * a + j) * P:(4 * a + j + 1) * P], ident[:])
                    last.then_inc(s["hT_done"], 1)

            def down(n):
                e = pe.value_load(meta[0:1, 0, bass.ds(n, 1)], min_val=0, max_val=EXPERTS - 1)
                for j in range(KF):
                    if j % 4 == 0:
                        pe.wait_ge(s["gelu_done"], 2 * n + j // 4 + 1)
                    last = mm(y_bank[:, 0:D], hTs[:, j, :],
                              w2s[:, bass.ds(KF * e + j, 1), :].rearrange("p a d -> p (a d)"),
                              start=j == 0, stop=j == KF - 1)
                last.then_inc(s["y_done"], 1)

            pe.wait_ge(s["meta_ready"], 1)
            pe.wait_ge(s["w1_in"], 16 * (EXPERTS + 1))
            pe.wait_ge(s["w2_in"], 16 * EXPERTS)
            xg_turn(0)
            up(0)
            xg_turn(1)
            with pe.Fori(0, BLOCKS - 2) as n:
                h_turn(n)
                up(n + 1)
                xg_turn(n + 2)
                down(n)
            h_turn(BLOCKS - 2)
            up(BLOCKS - 1)
            down(BLOCKS - 2)
            h_turn(BLOCKS - 1)
            down(BLOCKS - 1)

        @block.vector
        def _(dve):
            v = nc.vector
            prep = Steps(dve, s["meta_steps"])

            def centre(w, sums):
                w3 = w.rearrange("p (h d) -> p h d", d=HD)
                prep(v.tensor_reduce(sums, w3, AX.X, ALU.add))
                prep.sync()
                return v.scalar_tensor_tensor(
                    out=w3, in0=sums.unsqueeze(2).to_broadcast(w3.shape), scalar=-1.0 / HD,
                    in1=w3, op0=ALU.mult, op1=ALU.add)

            v.memset(on[:, 0, :], 0.0).then_inc(s["prep"], 1)
            prep(v.memset(kz, 0.0))
            for b in range(BATCH):
                prep(v.memset(vaug[b][:], 1.0))
            prep(v.memset(cum[:], 0.0))
            dve.wait_ge(s["wkv_in"], 16)
            dve.wait_ge(s["const_in"], 96)
            prep(centre(wkv[:, 0, 0:D], wsum[:, 0:16]))
            prep(centre(bkv[:, 0:D], wsum[0:KEYS, 16:32]))
            centre(wkv[:, 1, 0:D], wsum[:, 32:48]).then_inc(s["prep"], 1)
            prep.sync()
            dve.wait_ge(s["prep"], 2)

            def context(b):
                dve.wait_ge(s["kv_done"], b + 1)
                if b:
                    dve.wait_ge(s["kzT_done"], 3)
                v.tensor_tensor(kc, tail_bank[0:KEYS, 0:D], bkv[:, 0:D], ALU.add).then_inc(s["kc_ready"], 1)
                prep(v.tensor_tensor(vaug[b][:, :, 0:HD],
                                     tail_bank[0:KEYS, D:2 * D].rearrange("p (h d) -> p h d", d=HD),
                                     bkv[:, D:2 * D].rearrange("p (h d) -> p h d", d=HD), ALU.add))
                dve.wait_ge(s["ksq_done"], b + 1)
                prep(v.tensor_reduce(krs, ksq.rearrange("p (h d) -> p h d", d=HD), AX.X, ALU.add))
                prep.sync()
                v.tensor_scalar(krs, krs, 1.0 / HD, HEAD_EPS, ALU.mult, ALU.add).then_inc(s["kvar_ready"], 1)
                dve.wait_ge(s["krs_ready"], b + 1)
                k3 = kc.rearrange("p (h d) -> p h d", d=HD)
                prep(v.tensor_tensor(k3, k3, krs.unsqueeze(2).to_broadcast(k3.shape), ALU.mult))
                prep.sync()
                prep(v.tensor_tensor(k3, k3, hw[0:KEYS, 2:3, :].to_broadcast(k3.shape), ALU.mult))
                prep.sync()
                for c in range(KD):
                    flat = kz[:, HPC * c:HPC * (c + 1), :].rearrange("p h n -> p (h n)")
                    for h in range(HPC):
                        last = v.tensor_tensor(flat[:, h * (P + HD):h * (P + HD) + HD],
                                               k3[:, HPC * c + h, :], hw[0:KEYS, 3, :], ALU.add)
                        prep(last)
                prep.sync()
                v.memset(gs[:, 3, :], 0.0).then_inc(s["kz_ready"], 1)
                dve.wait_ge(s["kz_ready"], b + 1)
                v.memset(gs[:, 3, :], 0.0).then_inc(s["ctx_ready"], 1)
                dve.wait_ge(s["ctx_ready"], b + 1)

            context(0)
            context(1)

            dve.wait_ge(s["wq_in"], 32)
            prep(centre(wq[:, 0, :], wsum[:, 48:64]))
            prep(centre(bq[:], wsum[:, 64:80]))
            centre(wq[:, 1, :], wsum[:, 80:96]).then_inc(s["prep"], 1)
            for n in range(2):
                two = hw[:, n, :].rearrange("p (n two) -> p n two", two=2)
                prep(v.tensor_copy(hws[:, n, :].rearrange("p (n two) -> p n two", two=2), two[:, :, ::-1]))
            prep.sync()
            dve.wait_ge(s["rope_in"], 32)
            tab = [P, TILES, HD]
            prep(v.tensor_tensor(ropeb[:], sinw[:], hws[:, 1:2, :].to_broadcast(tab), ALU.mult))
            prep.sync()
            prep(v.tensor_tensor(sinw[:], sinw[:], hws[:, 0:1, :].to_broadcast(tab), ALU.mult))
            cosb = probs[:, 0, :].rearrange("p (t d) -> p t d", d=HD)
            dve.wait_ge(s["kzT_done"], 6)
            prep(v.tensor_tensor(cosb, cosw[:], hw[:, 1:2, :].to_broadcast(tab), ALU.mult))
            prep.sync()
            prep(v.tensor_tensor(ropeb[:], ropeb[:], cosb, ALU.add))
            prep(v.tensor_tensor(cosw[:], cosw[:], hw[:, 0:1, :].to_broadcast(tab), ALU.mult))
            prep.sync()
            prep_steps = prep.n

            def normalise(c, n, src, dst, which, ready):
                for j in range(2):
                    c(v.bn_stats(bst[:, j, 0, 0:6], src(j)))
                c.sync()
                settled(dve)
                for j in range(2):
                    c(v.bn_aggr(bst[:, j, 1, 0:2], bst[:, j, 0, 0:6]))
                c.sync()
                v.tensor_scalar(bst[:, :, 1, 2:3], bst[:, :, 1, 1:2], LN_EPS, None, ALU.add
                                ).then_inc(s[which + "var_ready"], 1)
                dve.wait_ge(s[which + "rs_ready"], n + 1)
                for j in range(2):
                    v.tensor_scalar(dst[:, j, :], src(j), bst[:, j, 1, 0:1], bst[:, j, 1, 2:3],
                                    ALU.subtract, ALU.mult).then_inc(s[ready], 1)

            def query(f, c):
                dve.wait_ge(s["q_done"], f + 1)
                v.tensor_tensor(qc[:], front_bank[:].rearrange("p (a n) -> p a n", a=2),
                                bq[:].unsqueeze(1).to_broadcast([P, 2, D]), ALU.add).then_inc(s["qc_ready"], 1)
                dve.wait_ge(s["qsq_done"], f + 1)
                c(v.tensor_reduce(qrs[:], qs[:].rearrange("p a (h d) -> p (a h) d", d=HD), AX.X, ALU.add))
                c.sync()
                v.tensor_scalar(qrs[:], qrs[:], 1.0 / HD, HEAD_EPS, ALU.mult, ALU.add).then_inc(s["qvar_ready"], 1)
                dve.wait_ge(s["qc_ready"], f + 1)
                dve.wait_ge(s["qrs_ready"], f + 1)
                q3 = qc[:].rearrange("p a (h d) -> p (a h) d", d=HD)
                c(v.tensor_tensor(q3, q3, qrs[:].unsqueeze(2).to_broadcast(q3.shape), ALU.mult))
                c.sync()
                for j in range(2):
                    q2 = qc[:, j, :].rearrange("p (h n two) -> p h n two", two=2, n=HD // 2)
                    o2 = qs[:, j, :].rearrange("p (h n two) -> p h n two", two=2, n=HD // 2)
                    sw = sinw[:, bass.ds(2 * f + j, 1), :].rearrange("p a (n two) -> p a n two", two=2)
                    for two in range(2):
                        c(v.tensor_tensor(o2[:, :, :, two], q2[:, :, :, 1 - two],
                                          sw[:, :, :, two].to_broadcast([P, HEADS, HD // 2]), ALU.mult))
                    c(v.tensor_tensor(qr[:, j, :].rearrange("p (h d) -> p h d", d=HD),
                                      qc[:, j, :].rearrange("p (h d) -> p h d", d=HD),
                                      cosw[:, bass.ds(2 * f + j, 1), :].to_broadcast([P, HEADS, HD]), ALU.mult))
                c.sync()
                for j in range(2):
                    s3 = qs[:, j, :].rearrange("p (h d) -> p h d", d=HD)
                    c(v.tensor_tensor(s3, s3, ropeb[:, bass.ds(2 * f + j, 1), :].to_broadcast([P, HEADS, HD]),
                                      ALU.add))
                c.sync()
                v.tensor_tensor(qr[:], qr[:], qs[:], ALU.add).then_inc(s["qr_ready"], 1)

            def maxima(f, j):
                for n in range(4):
                    dve.wait_ge(s["s_done"], 8 * f + 4 * j + n + 1)
                    v.tensor_reduce(mx[:, j, 4 * n:4 * n + 4],
                                    max_banks[n % 2][:, 0:4 * KEYS].rearrange("p (h n) -> p h n", n=KEYS),
                                    AX.X, ALU.max).then_inc(s["max_done"], 1)

            def split_max(f, c):
                dve.wait_ge(s["max_done"], 8 * f + 8)
                c(v.tensor_copy(m2[:, :, 0, :], mx[:]))
                c.sync()
                v.tensor_tensor(m2[:, :, 1, :], mx[:], m2[:, :, 0, :], ALU.subtract).then_inc(s["m2_ready"], 1)

            def output(t, c):
                dve.wait_ge(s["pv_done"], 8 * t + 8)
                for j in range(2):
                    o3 = pv_banks[j][:, 0:HEADS * (HD + 1)].rearrange("p (h d) -> p h d", d=HD + 1)
                    c(v.reciprocal(rden[:, j, :].unsqueeze(2), o3[:, :, HD:HD + 1]))
                c.sync()
                for j in range(2):
                    o3 = pv_banks[j][:, 0:HEADS * (HD + 1)].rearrange("p (h d) -> p h d", d=HD + 1)
                    v.tensor_tensor(on[:, j, :].rearrange("p (h d) -> p h d", d=HD), o3[:, :, 0:HD],
                                    rden[:, j, :].unsqueeze(2).to_broadcast([P, HEADS, HD]), ALU.mult
                                    ).then_inc(s["o_ready"], 1)

            def residual(t, c):
                dve.wait_ge(s["a_done"], t + 1)
                xs = xall[:, bass.ds(2 * t, 2), :]
                c(v.tensor_tensor(xs, xs, bo[:].unsqueeze(1).to_broadcast([P, 2, D]), ALU.add))
                c.sync()
                for j in range(2):
                    xj = xall[:, bass.ds(2 * t + j, 1), :].rearrange("p a d -> p (a d)")
                    v.tensor_tensor(xj, xj, tail_bank[:, j * D:(j + 1) * D], ALU.add).then_inc(s["x1_ready"], 1)
                dve.wait_ge(s["x1_ready"], 2 * t + 2)
                dve.wait_ge(s["xn2_stored"], 16 * t + 16)
                settled(dve)
                normalise(c, t, lambda j: xall[:, bass.ds(2 * t + j, 1), :].rearrange("p a d -> p (a d)"),
                          xn2, "x1", "xn2_ready")

            def logits_of():
                return tail_bank[:, 0:2 * EXPERTS].rearrange("p (a e) -> p a e", a=2)

            def spread(ap):
                return ap.unsqueeze(2).to_broadcast([P, 2, EXPERTS])

            def each(n):
                return expert[:, n:n + 1, :].to_broadcast([P, 2, EXPERTS])

            def top2(t, c):
                dve.wait_ge(s["logits_done"], t + 1)
                c(v.tensor_reduce(gs[:, 0, :], logits_of(), AX.X, ALU.max))
                c.sync()
                v.tensor_tensor(lsub[:], logits_of(), spread(gs[:, 0, :]), ALU.subtract
                                ).then_inc(s["lsub_ready"], 1)
                dve.wait_ge(s["gexp_done"], t + 1)
                for k in range(2):
                    src = (pg, pg2)[k]
                    c(v.tensor_reduce(top[:, :, k], src[:], AX.X, ALU.max))
                    c.sync()
                    c(v.tensor_tensor(same[:], src[:], spread(top[:, :, k]), ALU.is_equal))
                    c.sync()
                    c(v.scalar_tensor_tensor(out=cand[:], in0=same[:], scalar=-float(EXPERTS), in1=each(0),
                                             op0=ALU.mult, op1=ALU.add))
                    c.sync()
                    c(v.tensor_reduce(first[:, :, k], cand[:], AX.X, ALU.min))
                    c.sync()
                    c(v.tensor_tensor(onehot[:, :, k, :], each(1), spread(first[:, :, k]), ALU.is_equal))
                    c.sync()
                    if k == 0:
                        c(v.scalar_tensor_tensor(out=pg2[:], in0=onehot[:, :, 0, :], scalar=-2.0, in1=pg[:],
                                                 op0=ALU.mult, op1=ALU.add))
                        c.sync()
                c(v.tensor_copy(cum[:, 0, :], cum[:, 2, :]))
                c(v.tensor_tensor(mask[:], onehot[:, :, 0, :], onehot[:, :, 1, :], ALU.add))
                c.sync()
                c(v.tensor_tensor(cum[:, 1, :], cum[:, 0, :], mask[:, 0, :], ALU.add))
                c.sync()
                v.tensor_tensor(cum[:, 2, :], cum[:, 1, :], mask[:, 1, :], ALU.add).then_inc(s["mask_ready"], 1)
                c(v.tensor_reduce(gs[:, 1, :], top[:], AX.X, ALU.add))
                c.sync()
                c(v.reciprocal(gs[:, 2, :], gs[:, 1, :]))
                c.sync()

            def slot_entries(t, c):
                dve.wait_ge(s["rank_done"], t + 1)
                dve.wait_ge(s["entries_written"], t + 1)
                c(v.tensor_tensor(pos[:], tail_bank[:, 64:64 + 2 * EXPERTS].rearrange("p (a e) -> p a e", a=2),
                                  each(2), ALU.add))
                c(v.tensor_tensor(entry[:].bitcast(F32)[:, :, :, 1], top[:],
                                  gs[:, 2, :].unsqueeze(2).to_broadcast([P, 2, 2]), ALU.mult))
                c(v.tensor_copy(entry[:, :, :, 0],
                                tokens[:, bass.ds(2 * t, 2)].unsqueeze(2).to_broadcast([P, 2, 2])))
                c.sync()
                c(v.tensor_tensor(posk[:], onehot[:], pos[:].unsqueeze(2).to_broadcast([P, 2, 2, EXPERTS]), ALU.mult))
                c.sync()
                with nc.allow_low_precision(reason="a sum of one whole number and zeros"):
                    v.tensor_reduce(slots[:], posk[:], AX.X, ALU.add).then_inc(s["slots_ready"], 1)

            def step(i, b, front=False, back=False, tail=False):
                f, t = i + 1, i - 1
                cf = Steps(dve, s["front_steps"], FRONT_STEPS * f)
                ct = Steps(dve, s["tail_steps"], TAIL_STEPS * t)
                if tail:
                    output(t, ct)
                if front:
                    normalise(cf, f, lambda j: xall[:, bass.ds(2 * f + j, 1), :].rearrange("p a d -> p (a d)"),
                              xn, "x", "xn_ready")
                    query(f, cf)
                if tail:
                    residual(t, ct)
                if front:
                    maxima(f, 0)
                if tail:
                    top2(t, ct)
                if front:
                    maxima(f, 1)
                    split_max(f, cf)
                    assert cf.n == FRONT_STEPS, cf.n
                if tail:
                    slot_entries(t, ct)
                    assert ct.n == TAIL_STEPS, ct.n

            dve.wait_ge(s["x_first"], 16)
            dve.wait_ge(s["x_rest"], 16)
            dve.wait_ge(s["wo_in"], 16 * 9)
            dve.wait_ge(s["xn2_stored"], 16)
            dve.wait_ge(s["acc_stored"], 16)
            steps(dve, step)

            dve.wait_ge(s["mask_ready"], PAIRS)
            v.tensor_copy(nblk[:, 0, 0:1], nblk[:, 0, 0:1]) if False else None
            v.memset(gs[:, 3, :], 0.0).then_inc(s["cum_ready"], 1)
            dve.wait_ge(s["count_done"], 1)
            m = Steps(dve, s["meta_steps"], prep_steps)
            m(v.tensor_scalar(nblki[:, 0, :], tail_bank[0:1, 128:128 + EXPERTS], float(P - 1), None, ALU.add))
            m.sync()
            m(v.tensor_scalar(nblki[:, 1, :], nblki[:, 0, :], P.bit_length() - 1, None, ALU.arith_shift_right))
            m.sync()
            m(v.tensor_copy(nblk[:, 0, :], nblki[:, 1, :]))
            m(v.memset(metaf[:, 2, :], 1.0))
            m.sync()
            m(v.tensor_tensor_scan(nblk[:, 1, :], metaf[:, 2, 0:EXPERTS], nblk[:, 0, :], 0.0, ALU.mult, ALU.add))
            m.sync()
            wide = [1, BLOCKS, EXPERTS - 1]
            ends = nblk[:, 1:2, 0:EXPERTS - 1].to_broadcast(wide)
            m(v.tensor_tensor(ge, blockid[:].unsqueeze(2).to_broadcast(wide), ends, ALU.is_ge))
            m.sync()
            m(v.tensor_tensor(gep, ge, ends, ALU.mult))
            m(v.tensor_reduce(metaf[:, 0, :], ge, AX.X, ALU.add))
            m.sync()
            m(v.tensor_reduce(metaf[:, 1, :], gep, AX.X, ALU.max))
            m(v.tensor_copy(meta[:, 0, :], metaf[:, 0, :]))
            m.sync()
            m(v.tensor_tensor(metaf[:, 2, :], blockid[:], metaf[:, 1, :], ALU.subtract))
            m.sync()
            m(v.tensor_scalar(metaf[:, 1, :], metaf[:, 0, :], float(TOKENS // P), None, ALU.mult))
            m.sync()
            m(v.tensor_tensor(metaf[:, 2, :], metaf[:, 2, :], metaf[:, 1, :], ALU.add))
            m.sync()
            v.tensor_scalar(meta[:, 1, :], metaf[:, 2, :], float(P), None, ALU.mult).then_inc(s["meta_ready"], 1)

            def turned(n):
                dve.wait_ge(s["xgT_done"], n + 1)
                v.tensor_copy(xgTs.rearrange("p k n -> p (k n)"), xg_bank[:, 0:D]).then_inc(s["xgTs_ready"], 1)

            def bias(n):
                e = dve.value_load(meta[0:1, 0, bass.ds(n, 1)], min_val=0, max_val=EXPERTS - 1)
                for a in range(2):
                    dve.wait_ge(s["hT_done"], 2 * n + a + 1)
                    v.tensor_tensor(hbT[:, 4 * a:4 * a + 4, :], hT_banks[a][:].rearrange("p (j n) -> p j n", n=P),
                                    b1s[:, bass.ds(KF * e + 4 * a, 4)].unsqueeze(2).to_broadcast([P, 4, P]),
                                    ALU.add).then_inc(s["hbT_ready"], 1)

            def result(n):
                c = Steps(dve, s["block_steps"], BLOCK_STEPS * n)
                e = dve.value_load(meta[0:1, 0, bass.ds(n, 1)], min_val=0, max_val=EXPERTS - 1)
                dve.wait_ge(s["y_done"], n + 1)
                c(v.tensor_tensor(yb, y_bank[:, 0:D], b2s[:, bass.ds(e, 1), :].rearrange("p a d -> p (a d)"),
                                  ALU.add))
                if not (isinstance(n, int) and n == 0):
                    dve.wait_ge(s["added"], 16 * n)
                c(v.tensor_copy(sidx[:], table[:, bass.ds(n, 1), 0]))
                c.sync()
                c(v.tensor_scalar(ys, yb, table[:].bitcast(F32)[:, bass.ds(n, 1), 1], None, ALU.mult))
                c.sync()
                v.memset(gs[:, 3, :], 0.0).then_inc(s["y_ready"], 1)
                dve.wait_ge(s["y_ready"], n + 1)
                assert c.n == BLOCK_STEPS

            dve.wait_ge(s["meta_ready"], 1)
            dve.wait_ge(s["w1_in"], 16 * (EXPERTS + 1))
            dve.wait_ge(s["b2_in"], 16)
            dve.wait_ge(s["acc_stored"], 16 + 16 * PAIRS)
            turned(0)
            turned(1) if False else None
            bias(0)
            turned(1)
            result(0)
            with dve.Fori(1, BLOCKS - 1) as n:
                bias(n)
                turned(n + 1)
                result(n)
            bias(BLOCKS - 1)
            result(BLOCKS - 1)


def kernel(x, ctx_1024, L0_xattn_q_w, L0_xattn_q_b, L0_xattn_kv_w, L0_xattn_kv_b, L0_xattn_qn_w,
           L0_xattn_qn_b, L0_xattn_kn_w, L0_xattn_kn_b, L0_xattn_out_w, L0_xattn_out_b,
           L0_ffn_gate_w, L0_ffn_w1, L0_ffn_b1, L0_ffn_w2, L0_ffn_b2):
    import numpy as np
    import ml_dtypes
    import concourse.bacc as bacc
    from concourse.bass_utils import run_bass_kernel_spmd

    bf16 = ml_dtypes.bfloat16
    place, half = np.arange(SEQ, dtype=np.float32), np.arange(0, HD, 2, dtype=np.float32)
    angle = place[:, None] * (np.float32(1.0) / np.float32(10000.0) ** (half / np.float32(HD)))[None, :]
    scale = np.float32(HD ** -0.5)
    cos = np.repeat(np.cos(angle) * scale, 2, axis=1)
    sin = np.repeat(np.sin(angle) * scale, 2, axis=1)
    sin[:, 0::2] *= -1
    sel = np.zeros((2 * HEADS, HEADS, KEYS), bf16)
    for h in range(HEADS):
        sel[h, h, :] = sel[HEADS + h, h, :] = -1
    before = np.zeros((P, 2, P), bf16)
    before[:, 0, :] = np.triu(np.ones((P, P)), 1)
    before[:, 1, :] = 1
    slots = np.zeros((SLOTS, 2), np.int32)
    slots[:, 0] = TOKENS + np.arange(SLOTS) % P
    ids = np.arange(EXPERTS, dtype=np.float32)
    expert = np.broadcast_to(np.stack([ids, ids - EXPERTS, ids * TOKENS]), (P, 3, EXPERTS))

    arrays = [x, ctx_1024, np.transpose(L0_xattn_q_w), L0_xattn_q_b, np.transpose(L0_xattn_kv_w),
              L0_xattn_kv_b, L0_xattn_qn_w, L0_xattn_qn_b, L0_xattn_kn_w, L0_xattn_kn_b,
              np.transpose(L0_xattn_out_w), L0_xattn_out_b, L0_ffn_gate_w, L0_ffn_w1, L0_ffn_b1,
              L0_ffn_w2, L0_ffn_b2,
              np.eye(P, dtype=np.float32), np.eye(P).astype(bf16), before,
              np.tile(cos, (BATCH, 1)).astype(np.float32), np.tile(sin, (BATCH, 1)).astype(np.float32),
              sel, slots, np.arange(TOKENS, dtype=np.int32).reshape(TILES, P).T, expert,
              np.arange(BLOCKS, dtype=np.float32).reshape(1, BLOCKS)]
    nc = bacc.Bacc("TRN2", target_bir_lowering=False, num_devices=1)
    given, args = {}, []
    for n, a in enumerate(arrays):
        a = np.ascontiguousarray(a)
        given[f"in_{n}"] = a
        args.append(nc.dram_tensor(f"in_{n}", a.shape, mybir.dt.from_np(a.dtype), kind="ExternalInput").ap())
    args.append(nc.dram_tensor("out_0", (BATCH, SEQ, D), F32, kind="ExternalOutput").ap())
    xattn_moe_kernel(nc, *args)
    done = run_bass_kernel_spmd(nc, [given], core_ids=[0])
    return done.results[0]["out_0"]
```

```python
from contextlib import ExitStack

import concourse.bass as bass
from concourse import mybir

F32 = mybir.dt.float32
BF16 = mybir.dt.bfloat16
I32 = mybir.dt.int32
ALU = mybir.AluOpType
ACT = mybir.ActivationFunctionType
AX = mybir.AxisListType

P = 128
BATCH, SEQ, D = 2, 1024, 256
KEYS = 77
HEADS, HD = 16, 16
EXPERTS, FF = 8, 1024
TOKENS = BATCH * SEQ
TILES = TOKENS // P
PAIRS = TILES // 2
PAIRS_B = PAIRS // BATCH
KD = D // P
KF = FF // P
HPC = HEADS // KD
BLOCKS = 2 * TOKENS // P + EXPERTS - 1
SLOTS = (EXPERTS - 1) * TOKENS + BLOCKS * P
ROWS = TOKENS + P
LN_EPS, HEAD_EPS = 1e-5, 1e-6
FRONT_STEPS = 14
TAIL_STEPS = 7
ROUTE_STEPS = 21
BLOCK_STEPS = 3


class Steps:

    def __init__(self, eng, sem, base=0):
        self.eng, self.sem, self.base, self.n = eng, sem, base, 0

    def __call__(self, ins):
        ins.then_inc(self.sem, 1)
        self.n += 1

    def sync(self):
        self.eng.wait_ge(self.sem, self.base + self.n)


def xattn_moe_kernel(nc, x, ctx_in, wqT, q_b, wkvT, kv_b, qn_w, qn_b, kn_w, kn_b, woT, out_b,
                     gate_w, w1, b1, w2, b2, c_ident, c_identb, c_upper, c_cos, c_sin, c_sel,
                     c_slots, c_tokens, c_expert, c_block, out):
    x_v = x.rearrange("b (t p) d -> p (b t) d", p=P)
    out_rows = out.rearrange("b s d -> (b s) d")
    slot_table = nc.dram_tensor("slot_table", (SLOTS, 2), I32).ap()
    xn2_rows = nc.dram_tensor("xn2_rows", (ROWS, D), F32).ap()
    acc_rows = nc.dram_tensor("acc_rows", (ROWS, D), F32).ap()

    with ExitStack() as ctx:
        def sb(name, shape, dt=F32):
            return ctx.enter_context(nc.sbuf_tensor(name, shape, dt))

        def sem(name):
            return ctx.enter_context(nc.semaphore(name))

        banks = [ctx.enter_context(nc.psum_tensor(f"bank{n}", [P, 512], F32)) for n in range(8)]
        front_bank, tail_bank = banks[0], banks[1]
        max_banks, score_banks, pv_banks = banks[2:4], banks[4:6], banks[6:8]
        h_banks, hT_banks, y_bank, xg_bank = banks[4:6], banks[6:8], banks[2], banks[0]

        ident, identb = sb("ident", [P, P]), sb("identb", [P, P], BF16)
        upper = sb("upper", [P, 2, P], BF16)
        sel = sb("sel", [2 * HEADS, HEADS, KEYS], BF16)
        cosw, sinw, ropeb = (sb(n, [P, TILES, HD]) for n in ("cosw", "sinw", "ropeb"))
        hw = sb("hw", [P, 4, HD])
        hws = sb("hws", [P, 2, HD])
        tokens = sb("tokens", [P, TILES], I32)
        expert = sb("expert", [P, 3, EXPERTS])
        blockid = sb("blockid", [1, BLOCKS])
        wq, wo = sb("wq", [P, KD, D]), sb("wo", [P, KD, D])
        bq, bo = sb("bq", [P, D]), sb("bo", [P, D])
        gw = sb("gw", [P, KD, EXPERTS])
        w1s = sb("w1s", [P, EXPERTS * KD, FF])
        w2s = sb("w2s", [P, EXPERTS * KF, D])
        b1s = sb("b1s", [P, EXPERTS * KF])
        wsum = sb("wsum", [P, 2 * KD * HEADS + 2 * HEADS])

        kzT = [sb(f"kzT{b}", [P, HEADS, KEYS]) for b in range(BATCH)]
        vaug = [sb(f"vaug{b}", [KEYS, HEADS, HD + 1]) for b in range(BATCH)]
        xall = sb("xall", [P, TILES, D])
        probs = sb("probs", [P, HEADS, 2 * P])
        kz = probs[0:KEYS, 0:8, :].rearrange("p h (a n) -> p (h a) n", a=2)
        kc = probs[0:KEYS, 8, :]
        ksq = probs[0:KEYS, 9, :]
        cT = probs[:, 10, 0:KD * KEYS].rearrange("p (k n) -> p k n", k=KD)
        cin = probs[0:KEYS, 11, :]
        krs = sb("krs", [KEYS, HEADS])[:]
        power = sb("power", [P, 1])
        wkv = probs[:, 12:16, :].rearrange("p (k a) n -> p k (a n)", k=KD)
        bst = sb("bst", [P, 2, 2, 8])
        xn = sb("xn", [P, 2, D])
        xnTs = sb("xnTs", [P, 2, KD, P])
        qc = sb("qc", [P, 2, D])
        qs = sb("qs", [P, 2, D])
        bkv = qc[0:KEYS, :, :].rearrange("p a n -> p (a n)")
        qrs = sb("qrs", [P, 2 * HEADS])
        qr = xn
        qTs = sb("qTs", [P, KD, 2 * P])
        mx = sb("mx", [P, 2, HEADS])
        m2 = sb("m2", [P, 2, 2, HEADS], BF16)
        mTs = sb("mTs", [2 * HEADS, 2 * P], BF16)
        rden = sb("rden", [P, 2, HEADS])
        on = sb("on", [P, 2, D])
        oTs = sb("oTs", [P, 2, KD, P])
        xn2 = sb("xn2", [P, 2, D])
        xn2Ts = oTs
        lsub, pg = sb("lsub", [P, 2, EXPERTS]), sb("pg", [P, 2, EXPERTS])
        pg2 = sb("pg2", [P, 2, EXPERTS])
        cand, same = sb("cand", [P, 2, EXPERTS]), sb("same", [P, 2, EXPERTS])
        gs = sb("gs", [P, 4, 2])
        top = sb("top", [P, 2, 2])
        first = sb("first", [P, 2, 2])
        onehot = sb("onehot", [P, 2, 2, EXPERTS])
        mask = sb("mask", [P, 2, EXPERTS], BF16)
        cum = sb("cum", [P, 3, EXPERTS], BF16)
        pos = sb("pos", [P, 2, EXPERTS])
        posk = sb("posk", [P, 2, 2, EXPERTS])
        slots = sb("slots", [P, 2, 2], I32)
        entry = sb("entry", [P, 2, 2, 2], I32)
        nblk, nblki = sb("nblk", [1, 2, EXPERTS]), sb("nblki", [1, 2, EXPERTS], I32)
        ge, gep = (buf[0:1, :, :].rearrange("p a n -> p (a n)")[:, 0:BLOCKS * (EXPERTS - 1)]
                   .rearrange("p (b e) -> p b e", b=BLOCKS) for buf in (qc, qs))
        metaf = sb("metaf", [1, 3, BLOCKS])
        meta = sb("meta", [1, 2, BLOCKS], I32)
        table = sb("table", [P, BLOCKS, 2], I32)
        gidx, sidx = sb("gidx", [P, 1], I32), sb("sidx", [P, 1], I32)
        b2s = probs[:, 0:8, :]
        hTs = probs[:, 8:12, :].rearrange("p a (b n) -> p (a b) n", n=P)
        xg, yb, ys = probs[:, 12, :], probs[:, 13, :], probs[:, 14, :]
        xgTs = probs[:, 15, :].rearrange("p (k n) -> p k n", n=P)
        hs = xall[:, 0:4, :].rearrange("p t d -> p (t d)")
        hbT = xall[:, 4:8, :].rearrange("p t (a n) -> p (t a) n", n=P)

        names = """const_in rope_in wq_in wkv_in wo_in ctx_in0 ctx_in1 x_first x_rest w1_in w2_in b2_in
            paced power_ready kvar_ready krs_ready xvar_ready xrs_ready qvar_ready qrs_ready
            x1var_ready x1rs_ready prep cT_done cTs_ready kv_done kc_ready ksq_done kz_ready kzT_done kzT_ready
            ctx_ready front_steps tail_steps route_steps xn_ready xT_done xnTs_ready q_done qc_ready qsq_done
            qr_ready qT_done qTs_ready  s_done max_done m2_ready mT_done mTs_ready
            st_done exp_done pv_done o_ready oT_done oTs_ready a_done x1_ready xn2_ready xn2_stored
            acc_stored xn2T_done xn2Ts_ready logits_done lsub_ready gexp_done mask_ready rank_done
            slots_ready padded scattered entries_written cum_ready count_done meta_steps meta_ready
            table_in idx_ready gathered xgT_done xgTs_ready h_done hs_ready hT_done hbT_ready
            gelu_done y_done block_steps y_ready sidx_ready added out_stored""".split()
        s = {n: sem(n) for n in names}

        def settled(eng):
            eng.sem_inc(s["paced"], 1)

        def steps(eng, step):
            step(-1, 0, front=True)
            step(0, 0, front=True, back=True)
            step(1, 0, front=True, back=True, tail=True)
            with eng.Fori(2, PAIRS_B) as i:
                step(i, 0, front=True, back=True, tail=True, route=True)
            with eng.Fori(PAIRS_B, PAIRS - 1) as i:
                step(i, 1, front=True, back=True, tail=True, route=True)
            step(PAIRS - 1, 1, back=True, tail=True, route=True)
            step(PAIRS, 1, tail=True, route=True)
            step(PAIRS + 1, 1, route=True)

        block = ctx.enter_context(nc.Block())

        @block.sync
        def _(sp):
            sp.dma_start(cin, ctx_in[0]).then_inc(s["ctx_in0"], 16)
            sp.dma_start(wkv, wkvT.rearrange("(k p) n -> p k n", p=P)).then_inc(s["wkv_in"], 16)
            sp.dma_start(ident[:], c_ident).then_inc(s["const_in"], 16)
            sp.dma_start(bkv, kv_b.partition_broadcast(KEYS)).then_inc(s["const_in"], 16)
            for n, v in enumerate((qn_w, qn_b, kn_w, kn_b)):
                sp.dma_start(hw[:, n, :], v.partition_broadcast(P)).then_inc(s["const_in"], 16)
            sp.dma_start(xall[:, 0:2, :], x_v[:, 0:2, :]).then_inc(s["x_first"], 16)
            sp.dma_start(wq[:], wqT.rearrange("(k p) n -> p k n", p=P)).then_inc(s["wq_in"], 16)
            sp.dma_start(bq[:], q_b.partition_broadcast(P)).then_inc(s["wq_in"], 16)
            sp.dma_start(cosw[:], c_cos.rearrange("(t p) n -> p t n", p=P)).then_inc(s["rope_in"], 16)
            sp.dma_start(sinw[:], c_sin.rearrange("(t p) n -> p t n", p=P)).then_inc(s["rope_in"], 16)
            sp.dma_start(identb[:], c_identb).then_inc(s["wo_in"], 16)
            sp.dma_start(sel[:], c_sel).then_inc(s["wo_in"], 16)
            sp.dma_start(xall[:, 2:TILES, :], x_v[:, 2:TILES, :]).then_inc(s["x_rest"], 16)
            sp.dma_start(wo[:], woT.rearrange("(k p) n -> p k n", p=P)).then_inc(s["wo_in"], 16)
            sp.dma_start(bo[:], out_b.partition_broadcast(P)).then_inc(s["wo_in"], 16)
            sp.dma_start(gw[:], gate_w.rearrange("(k p) n -> p k n", p=P)).then_inc(s["wo_in"], 16)
            sp.dma_start(upper[:], c_upper).then_inc(s["wo_in"], 16)
            sp.dma_start(tokens[:], c_tokens).then_inc(s["wo_in"], 16)
            sp.dma_start(expert[:], c_expert).then_inc(s["wo_in"], 16)
            sp.dma_start(blockid[:], c_block).then_inc(s["wo_in"], 16)
            sp.dma_start(slot_table, c_slots).then_inc(s["padded"], 16)
            sp.wait_ge(s["prep"], 1)
            sp.dma_start(xn2_rows[TOKENS:ROWS, :], on[:, 0, :]).then_inc(s["xn2_stored"], 16)
            sp.dma_start(acc_rows[TOKENS:ROWS, :], on[:, 0, :]).then_inc(s["acc_stored"], 16)
            sp.wait_ge(s["ctx_ready"], 1)
            sp.dma_start(cin, ctx_in[1]).then_inc(s["ctx_in1"], 16)
            sp.dma_start(b1s[:], b1.rearrange("e (j p) -> p (e j)", p=P),
                         allow_slow_non_contiguous=True).then_inc(s["w1_in"], 16)

            def step(i, b, front=False, back=False, tail=False, route=False):
                t = i - 1
                if tail:
                    sp.wait_ge(s["x1_ready"], 2 * t + 2)
                    sp.dma_start(
                        acc_rows[0:TOKENS, :].rearrange("(t p) d -> p t d", p=P)[:, bass.ds(2 * t, 2), :],
                        xall[:, bass.ds(2 * t, 2), :]).then_inc(s["acc_stored"], 16)
                    sp.wait_ge(s["xn2_ready"], 2 * t + 2)
                    sp.dma_start(
                        xn2_rows[0:TOKENS, :].rearrange("(t p) d -> p t d", p=P)[:, bass.ds(2 * t, 2), :],
                        xn2[:]).then_inc(s["xn2_stored"], 16)

            steps(sp, step)
            sp.wait_ge(s["pv_done"], 8 * PAIRS)
            sp.dma_start(b2s, b2.partition_broadcast(P)).then_inc(s["b2_in"], 16)

            sp.wait_ge(s["entries_written"], 1 + PAIRS)
            sp.wait_ge(s["meta_ready"], 1)
            with sp.Fori(0, BLOCKS) as n:
                start = sp.value_load(meta[0:1, 1, bass.ds(n, 1)], min_val=0, max_val=SLOTS - P)
                sp.dma_start(table[:, bass.ds(n, 1), :],
                             slot_table[bass.ds(start, P), :].rearrange("p (a c) -> p a c", a=1)
                             ).then_inc(s["table_in"], 16)
                sp.wait_ge(s["table_in"], 16 * n + 16)
                settled(sp)
            sp.wait_ge(s["added"], 16 * BLOCKS)
            sp.dma_start(out_rows.rearrange("(a r) d -> a (r d)", a=P),
                         acc_rows[0:TOKENS, :].rearrange("(a r) d -> a (r d)", a=P)
                         ).then_inc(s["out_stored"], 16)
            sp.wait_ge(s["out_stored"], 16)

        @block.gpsimd
        def _(pool):
            def root(which, n, buf):
                pool.wait_ge(s[which + "var_ready"], n + 1)
                nc.gpsimd.tensor_tensor(buf, buf, power[0:buf.shape[0], :].to_broadcast(buf.shape), ALU.pow
                                        ).then_inc(s[which + "rs_ready"], 1)

            def step(i, front=False, tail=False, route=False):
                f, t, r = i + 1, i - 1, i - 2
                if front:
                    root("x", f, bst[:, :, 1, 2])
                    root("q", f, qrs[:])
                if tail:
                    root("x1", t, bst[:, :, 1, 2])
                if route:
                    pool.wait_ge(s["slots_ready"], r + 1)
                    settled(pool)
                    for j in range(2):
                        for k in range(2):
                            nc.gpsimd.indirect_dma_start(
                                slot_table, bass.IndirectOffsetOnAxis(ap=slots[:, j, k:k + 1], axis=0),
                                entry[:, j, k, :], None).then_inc(s["scattered"], 16)
                    pool.wait_ge(s["scattered"], 64 * r + 64)
                    pool.sem_inc(s["entries_written"], 1)

            nc.gpsimd.memset(power[:], -0.5).then_inc(s["power_ready"], 1)
            pool.wait_ge(s["power_ready"], 1)
            for b in range(BATCH):
                root("k", b, krs)
            pool.wait_ge(s["padded"], 16)
            pool.sem_inc(s["entries_written"], 1)
            step(-1, front=True)
            step(0, front=True)
            step(1, front=True, tail=True)
            with pool.Fori(2, PAIRS - 1) as i:
                step(i, front=True, tail=True, route=True)
            step(PAIRS - 1, tail=True, route=True)
            step(PAIRS, tail=True, route=True)
            step(PAIRS + 1, route=True)

            def gather(n):
                pool.wait_ge(s["table_in"], 16 * n + 16)
                settled(pool)
                nc.gpsimd.tensor_copy(gidx[:], table[:, bass.ds(n, 1), 0]).then_inc(s["idx_ready"], 1)
                pool.wait_ge(s["idx_ready"], n + 1)
                settled(pool)
                nc.gpsimd.indirect_dma_start(
                    xg, None, xn2_rows, bass.IndirectOffsetOnAxis(ap=gidx[:, 0:1], axis=0)
                ).then_inc(s["gathered"], 16)

            def add_back(n):
                settled(pool)
                nc.gpsimd.indirect_dma_start(
                    acc_rows, bass.IndirectOffsetOnAxis(ap=sidx[:, 0:1], axis=0), ys, None,
                    compute_op=ALU.add).then_inc(s["added"], 16)

            pool.wait_ge(s["xn2_stored"], 16 + 16 * PAIRS)
            pool.wait_ge(s["acc_stored"], 16 + 16 * PAIRS)
            gather(0)
            for n in range(1, 3):
                pool.wait_ge(s["xgT_done"], n)
                gather(n)
            with pool.Fori(0, BLOCKS - 3) as n:
                pool.wait_ge(s["xgT_done"], n + 3)
                gather(n + 3)
                pool.wait_ge(s["y_ready"], n + 1)
                add_back(n)
            for n in range(BLOCKS - 3, BLOCKS):
                pool.wait_ge(s["y_ready"], n + 1)
                add_back(n)

        @block.scalar
        def _(act):
            w1_v = w1.rearrange("e (k p) f -> p (e k) f", p=P)
            w2_v = w2.rearrange("e (j p) d -> p (e j) d", p=P)

            def context(b):
                act.wait_ge(s["cT_done"], b + 1)
                nc.scalar.copy(cT, front_bank[:, 0:KD * KEYS].rearrange("p (k n) -> p k n", k=KD)
                               ).then_inc(s["cTs_ready"], 1)
                act.wait_ge(s["kc_ready"], b + 1)
                nc.scalar.activation(ksq, kc, ACT.Square).then_inc(s["ksq_done"], 1)
                for n, (lo, hi) in enumerate(((0, 6), (6, 12), (12, HEADS))):
                    act.wait_ge(s["kzT_done"], 3 * b + n + 1)
                    nc.scalar.copy(kzT[b][:, lo:hi, :],
                                   (max_banks + score_banks)[n][:, 0:(hi - lo) * KEYS]
                                   .rearrange("p (h n) -> p h n", n=KEYS)).then_inc(s["kzT_ready"], 1)

            context(0)
            context(1)
            for e in range(EXPERTS):
                act.dma_start(w1s[:, KD * e:KD * e + KD, :], w1_v[:, KD * e:KD * e + KD, :]
                              ).then_inc(s["w1_in"], 16)
                act.dma_start(w2s[:, KF * e:KF * e + KF, :], w2_v[:, KF * e:KF * e + KF, :]
                              ).then_inc(s["w2_in"], 16)

            def exp(i, g):
                act.wait_ge(s["st_done"], 8 * i + g + 1)
                nc.scalar.activation(probs[0:KEYS, 2 * g:2 * g + 2, :],
                                     score_banks[g % 2][0:KEYS, :].rearrange("p (a n) -> p a n", a=2),
                                     ACT.Exp).then_inc(s["exp_done"], 1)

            def bank_to(buf, bank):
                return nc.scalar.copy(buf[:].rearrange("p a b n -> p (a b n)"), bank[:])

            def step(i, b, front=False, back=False, tail=False, route=False):
                f, t, r = i + 1, i - 1, i - 2
                if back:
                    exp(i, 0)
                    exp(i, 1)
                if front:
                    act.wait_ge(s["xT_done"], f + 1)
                    bank_to(xnTs, front_bank).then_inc(s["xnTs_ready"], 1)
                if back:
                    exp(i, 2)
                if route:
                    act.wait_ge(s["lsub_ready"], r + 1)
                    nc.scalar.activation(pg[:], lsub[:], ACT.Exp).then_inc(s["gexp_done"], 1)
                if front:
                    act.wait_ge(s["qc_ready"], f + 1)
                    nc.scalar.activation(qs[:], qc[:], ACT.Square).then_inc(s["qsq_done"], 1)
                if tail:
                    act.wait_ge(s["oT_done"], t + 1)
                    bank_to(oTs, tail_bank).then_inc(s["oTs_ready"], 1)
                if back:
                    for g in range(3, 8):
                        exp(i, g)
                if front:
                    act.wait_ge(s["qT_done"], f + 1)
                    nc.scalar.copy(qTs[:].rearrange("p c n -> p (c n)"), front_bank[:]
                                   ).then_inc(s["qTs_ready"], 1)
                if tail:
                    act.wait_ge(s["xn2T_done"], t + 1)
                    bank_to(xn2Ts, tail_bank).then_inc(s["xn2Ts_ready"], 1)
                if front:
                    act.wait_ge(s["mT_done"], f + 1)
                    nc.scalar.copy(mTs[:], front_bank[0:2 * HEADS, 0:P].bitcast(BF16)
                                   ).then_inc(s["mTs_ready"], 1)
            steps(act, step)

            def h_copy(n):
                for a in range(2):
                    act.wait_ge(s["h_done"], 2 * n + a + 1)
                    nc.scalar.copy(hs[:, 512 * a:512 * a + 512], h_banks[a][:]).then_inc(s["hs_ready"], 1)

            def gelu(n):
                for a in range(2):
                    act.wait_ge(s["hbT_ready"], 2 * n + a + 1)
                    nc.scalar.activation(hTs[:, 4 * a:4 * a + 4, :], hbT[:, 4 * a:4 * a + 4, :],
                                         ACT.Gelu).then_inc(s["gelu_done"], 1)

            h_copy(0)
            with act.Fori(0, BLOCKS - 1) as n:
                gelu(n)
                h_copy(n + 1)
            gelu(BLOCKS - 1)

        @block.tensor
        def _(pe):
            mm = nc.tensor.matmul

            def context(b):
                pe.wait_ge(s[f"ctx_in{b}"], 16)
                if b == 0:
                    pe.wait_ge(s["const_in"], 96)
                else:
                    pe.wait_ge(s["kc_ready"], 1)
                for k in range(KD):
                    last = nc.tensor.transpose(front_bank[:, k * KEYS:(k + 1) * KEYS],
                                               cin[:, k * P:(k + 1) * P], ident[0:KEYS, 0:KEYS])
                last.then_inc(s["cT_done"], 1)
                pe.wait_ge(s["cTs_ready"], b + 1)
                if b == 0:
                    pe.wait_ge(s["prep"], 2)
                for k in range(KD):
                    last = mm(tail_bank[0:KEYS, :], cT[:, k, :], wkv[:, k, :], start=k == 0, stop=k == KD - 1)
                last.then_inc(s["kv_done"], 1)
                pe.wait_ge(s["kz_ready"], b + 1)
                for n, (lo, hi) in enumerate(((0, 6), (6, 12), (12, HEADS))):
                    if b:
                        pe.wait_ge(s["kzT_ready"], n + 1)
                    for h in range(lo, hi):
                        last = nc.tensor.transpose(
                            (max_banks + score_banks)[n][:, (h - lo) * KEYS:(h - lo + 1) * KEYS],
                            kz[:, h, :], ident[0:KEYS, 0:KEYS])
                    last.then_inc(s["kzT_done"], 1)

            context(0)
            context(1)
            pe.wait_ge(s["kzT_ready"], 6)
            pe.wait_ge(s["ctx_ready"], 2)
            pe.wait_ge(s["prep"], 3)
            pe.wait_ge(s["wo_in"], 16 * 9)

            def scores(i, b, g):
                if g == 0:
                    pe.wait_ge(s["mTs_ready"], i + 1)
                if not (isinstance(i, int) and i == 0 and g < 2):
                    pe.wait_ge(s["exp_done"], 8 * i + g - 1)
                for a in range(2):
                    h = 2 * g + a
                    to = score_banks[g % 2][0:KEYS, a * 2 * P:(a + 1) * 2 * P]
                    mm(to, kzT[b][:, h, :], qTs[:, h // HPC, :], start=True, stop=False)
                    last = mm(to, sel[:, h, :], mTs[:], start=False, stop=True)
                last.then_inc(s["st_done"], 1)

            def values(i, b, g):
                pe.wait_ge(s["exp_done"], 8 * i + g + 1)
                if g == 0 and not (isinstance(i, int) and i == 0):
                    pe.wait_ge(s["o_ready"], 2 * i)
                for j in range(2):
                    for h in (2 * g, 2 * g + 1):
                        last = mm(pv_banks[j][:, h * (HD + 1):(h + 1) * (HD + 1)],
                                  probs[0:KEYS, h, j * P:(j + 1) * P], vaug[b][:, h, :],
                                  start=True, stop=True)
                last.then_inc(s["pv_done"], 1)

            def maxima(f, j):
                n = 0
                if j == 0:
                    pe.wait_ge(s["qTs_ready"], f + 1)
                kb = kz_of(f)
                for c in range(KD):
                    for g in range(2):
                        if not (isinstance(f, int) and f == 0 and j == 0 and n < 2):
                            pe.wait_ge(s["max_done"], 8 * f + 4 * j + n - 1)
                        mm(max_banks[n % 2][:, 0:4 * KEYS], qTs[:, c, j * P:(j + 1) * P],
                           kb[:, HPC * c + 4 * g:HPC * c + 4 * g + 4, :].rearrange("p h n -> p (h n)"),
                           start=True, stop=True).then_inc(s["s_done"], 1)
                        n += 1

            front_batch = [0]

            def kz_of(f):
                return kzT[front_batch[0]]

            def transposes(bank, src, split):
                for j in range(2):
                    for k in range(KD):
                        at = (2 * j + k if split else 2 * k + j) * P
                        last = nc.tensor.transpose(bank[:, at:at + P], src[:, j, k * P:(k + 1) * P], ident[:])
                return last

            def project(bank, lhs, w, n):
                for j in range(2):
                    for k in range(KD):
                        last = mm(bank[:, j * n:(j + 1) * n], lhs[:, j, k, :], w[:, k, :],
                                  start=k == 0, stop=k == KD - 1)
                return last

            def step(i, b, front=False, back=False, tail=False, route=False):
                f, t, r = i + 1, i - 1, i - 2
                if route:
                    pe.wait_ge(s["xn2Ts_ready"], r + 1)
                    project(max_banks[0], xn2Ts, gw, EXPERTS).then_inc(s["logits_done"], 1)
                if back:
                    scores(i, b, 0)
                    scores(i, b, 1)
                if front:
                    pe.wait_ge(s["xn_ready"], 2 * f + 2)
                    if back:
                        pe.wait_ge(s["mTs_ready"], f)
                    transposes(front_bank, xn, True).then_inc(s["xT_done"], 1)
                if back:
                    scores(i, b, 2)
                if front:
                    pe.wait_ge(s["xnTs_ready"], f + 1)
                    project(front_bank, xnTs, wq, D).then_inc(s["q_done"], 1)
                if tail:
                    pe.wait_ge(s["o_ready"], 2 * t + 2)
                    transposes(tail_bank, on, True).then_inc(s["oT_done"], 1)
                if back:
                    scores(i, b, 3)
                if tail:
                    pe.wait_ge(s["oTs_ready"], t + 1)
                    project(tail_bank, oTs, wo, D).then_inc(s["a_done"], 1)
                if back:
                    scores(i, b, 4)
                    scores(i, b, 5)
                if route:
                    pe.wait_ge(s["mask_ready"], r + 1)
                    for j in range(2):
                        to = max_banks[1][:, j * EXPERTS:(j + 1) * EXPERTS]
                        mm(to, upper[:, 0, :], mask[:, j, :], start=True, stop=False)
                        last = mm(to, upper[:, 1, :], cum[:, j, :], start=False, stop=True)
                    last.then_inc(s["rank_done"], 1)
                if back:
                    for g in range(6, 8):
                        scores(i, b, g)
                    for g in range(3):
                        values(i, b, g)
                if front:
                    pe.wait_ge(s["qr_ready"], 2 * f + 2)
                    transposes(front_bank, qr, False).then_inc(s["qT_done"], 1)
                if back:
                    values(i, b, 3)
                if front:
                    if route:
                        pe.wait_ge(s["slots_ready"], r + 1)
                    maxima(f, 0)
                if tail:
                    pe.wait_ge(s["xn2_ready"], 2 * t + 2)
                    transposes(tail_bank, xn2, True).then_inc(s["xn2T_done"], 1)
                if back:
                    values(i, b, 4)
                if front:
                    maxima(f, 1)
                if back:
                    values(i, b, 5)
                if front:
                    pe.wait_ge(s["m2_ready"], f + 1)
                    for j in range(2):
                        last = nc.tensor.transpose(
                            front_bank[0:2 * HEADS, j * P // 2:(j + 1) * P // 2].bitcast(BF16),
                            m2[:, j, :, :].rearrange("p a h -> p (a h)"), identb[:])
                    last.then_inc(s["mT_done"], 1)
                if back:
                    values(i, b, 6)
                    values(i, b, 7)
            step(-1, 0, front=True)
            step(0, 0, front=True, back=True)
            step(1, 0, front=True, back=True, tail=True)
            step(2, 0, front=True, back=True, tail=True, route=True)
            front_batch[0] = 1
            step(3, 0, front=True, back=True, tail=True, route=True)
            with pe.Fori(PAIRS_B, PAIRS - 1) as i:
                step(i, 1, front=True, back=True, tail=True, route=True)
            step(PAIRS - 1, 1, back=True, tail=True, route=True)
            step(PAIRS, 1, tail=True, route=True)
            step(PAIRS + 1, 1, route=True)
            pe.wait_ge(s["cum_ready"], 1)
            mm(tail_bank[:, 128:128 + EXPERTS], upper[:, 1, :], cum[:, 2, :], start=True, stop=True
               ).then_inc(s["count_done"], 1)

            def xg_turn(n):
                pe.wait_ge(s["gathered"], 16 * n + 16)
                for k in range(KD):
                    last = nc.tensor.transpose(xg_bank[:, k * P:(k + 1) * P], xg[:, k * P:(k + 1) * P], ident[:])
                last.then_inc(s["xgT_done"], 1)

            def expert_of(n):
                return pe.value_load(meta[0:1, 0, bass.ds(n, 1)], min_val=0, max_val=EXPERTS - 1)

            def up(n, e):
                pe.wait_ge(s["xgTs_ready"], n + 1)
                for a in range(2):
                    for k in range(KD):
                        last = mm(h_banks[a][:], xgTs[:, k, :],
                                  w1s[:, bass.ds(KD * e + k, 1), 512 * a:512 * a + 512].rearrange("p a f -> p (a f)"),
                                  start=k == 0, stop=k == KD - 1)
                    last.then_inc(s["h_done"], 1)

            def h_turn(n):
                for a in range(2):
                    pe.wait_ge(s["hs_ready"], 2 * n + a + 1)
                    for j in range(4):
                        last = nc.tensor.transpose(hT_banks[a][:, j * P:(j + 1) * P],
                                                   hs[:, (4 * a + j) * P:(4 * a + j + 1) * P], ident[:])
                    last.then_inc(s["hT_done"], 1)

            def down(n, e):
                for j in range(KF):
                    if j % 4 == 0:
                        pe.wait_ge(s["gelu_done"], 2 * n + j // 4 + 1)
                    last = mm(y_bank[:, 0:D], hTs[:, j, :],
                              w2s[:, bass.ds(KF * e + j, 1), :].rearrange("p a d -> p (a d)"),
                              start=j == 0, stop=j == KF - 1)
                last.then_inc(s["y_done"], 1)

            pe.wait_ge(s["meta_ready"], 1)
            pe.wait_ge(s["w1_in"], 16 * (EXPERTS + 1))
            pe.wait_ge(s["w2_in"], 16 * EXPERTS)
            xg_turn(0)
            up(0, expert_of(0))
            pe.wait_ge(s["xgTs_ready"], 1)
            xg_turn(1)
            with pe.Fori(0, BLOCKS - 2) as n:
                e, e_next = expert_of(n), expert_of(n + 1)
                h_turn(n)
                up(n + 1, e_next)
                xg_turn(n + 2)
                down(n, e)
            for n in range(BLOCKS - 2, BLOCKS):
                h_turn(n)
                if n + 1 < BLOCKS:
                    up(n + 1, expert_of(n + 1))
                down(n, expert_of(n))

        @block.vector
        def _(dve):
            v = nc.vector
            prep = Steps(dve, s["meta_steps"])

            def centre(w, sums):
                w3 = w.rearrange("p (h d) -> p h d", d=HD)
                prep(v.tensor_reduce(sums, w3, AX.X, ALU.add))
                prep.sync()
                return v.scalar_tensor_tensor(
                    out=w3, in0=sums.unsqueeze(2).to_broadcast(w3.shape), scalar=-1.0 / HD,
                    in1=w3, op0=ALU.mult, op1=ALU.add)

            v.memset(on[:, 0, :], 0.0).then_inc(s["prep"], 1)
            prep(v.memset(kz, 0.0))
            for b in range(BATCH):
                prep(v.memset(vaug[b][:], 1.0))
            prep(v.memset(cum[:], 0.0))
            dve.wait_ge(s["wkv_in"], 16)
            dve.wait_ge(s["const_in"], 96)
            prep(centre(wkv[:, 0, 0:D], wsum[:, 0:16]))
            prep(centre(bkv[:, 0:D], wsum[0:KEYS, 16:32]))
            centre(wkv[:, 1, 0:D], wsum[:, 32:48]).then_inc(s["prep"], 1)
            prep.sync()
            dve.wait_ge(s["prep"], 2)

            def context(b):
                dve.wait_ge(s["kv_done"], b + 1)
                if b:
                    dve.wait_ge(s["kzT_done"], 3)
                v.tensor_tensor(kc, tail_bank[0:KEYS, 0:D], bkv[:, 0:D], ALU.add).then_inc(s["kc_ready"], 1)
                prep(v.tensor_tensor(vaug[b][:, :, 0:HD],
                                     tail_bank[0:KEYS, D:2 * D].rearrange("p (h d) -> p h d", d=HD),
                                     bkv[:, D:2 * D].rearrange("p (h d) -> p h d", d=HD), ALU.add))
                dve.wait_ge(s["ksq_done"], b + 1)
                prep(v.tensor_reduce(krs, ksq.rearrange("p (h d) -> p h d", d=HD), AX.X, ALU.add))
                prep.sync()
                v.tensor_scalar(krs, krs, 1.0 / HD, HEAD_EPS, ALU.mult, ALU.add).then_inc(s["kvar_ready"], 1)
                dve.wait_ge(s["krs_ready"], b + 1)
                k3 = kc.rearrange("p (h d) -> p h d", d=HD)
                prep(v.tensor_tensor(k3, k3, krs.unsqueeze(2).to_broadcast(k3.shape), ALU.mult))
                prep.sync()
                prep(v.tensor_tensor(k3, k3, hw[0:KEYS, 2:3, :].to_broadcast(k3.shape), ALU.mult))
                prep.sync()
                for c in range(KD):
                    flat = kz[:, HPC * c:HPC * (c + 1), :].rearrange("p h n -> p (h n)")
                    for h in range(HPC):
                        last = v.tensor_tensor(flat[:, h * (P + HD):h * (P + HD) + HD],
                                               k3[:, HPC * c + h, :], hw[0:KEYS, 3, :], ALU.add)
                        prep(last)
                prep.sync()
                v.memset(gs[:, 3, :], 0.0).then_inc(s["kz_ready"], 1)
                dve.wait_ge(s["kz_ready"], b + 1)
                v.memset(gs[:, 3, :], 0.0).then_inc(s["ctx_ready"], 1)
                dve.wait_ge(s["ctx_ready"], b + 1)

            context(0)
            context(1)

            dve.wait_ge(s["wq_in"], 32)
            prep(centre(wq[:, 0, :], wsum[:, 48:64]))
            prep(centre(bq[:], wsum[:, 64:80]))
            centre(wq[:, 1, :], wsum[:, 80:96]).then_inc(s["prep"], 1)
            for n in range(2):
                two = hw[:, n, :].rearrange("p (n two) -> p n two", two=2)
                prep(v.tensor_copy(hws[:, n, :].rearrange("p (n two) -> p n two", two=2), two[:, :, ::-1]))
            prep.sync()
            dve.wait_ge(s["rope_in"], 32)
            tab = [P, TILES, HD]
            prep(v.tensor_tensor(ropeb[:], sinw[:], hws[:, 1:2, :].to_broadcast(tab), ALU.mult))
            prep.sync()
            prep(v.tensor_tensor(sinw[:], sinw[:], hws[:, 0:1, :].to_broadcast(tab), ALU.mult))
            cosb = probs[:, 0, :].rearrange("p (t d) -> p t d", d=HD)
            dve.wait_ge(s["kzT_done"], 6)
            prep(v.tensor_tensor(cosb, cosw[:], hw[:, 1:2, :].to_broadcast(tab), ALU.mult))
            prep.sync()
            prep(v.tensor_tensor(ropeb[:], ropeb[:], cosb, ALU.add))
            prep(v.tensor_tensor(cosw[:], cosw[:], hw[:, 0:1, :].to_broadcast(tab), ALU.mult))
            prep.sync()
            prep_steps = prep.n

            def normalise(c, n, src, dst, which, ready):
                for j in range(2):
                    c(v.bn_stats(bst[:, j, 0, 0:6], src(j)))
                c.sync()
                settled(dve)
                for j in range(2):
                    c(v.bn_aggr(bst[:, j, 1, 0:2], bst[:, j, 0, 0:6]))
                c.sync()
                v.tensor_scalar(bst[:, :, 1, 2:3], bst[:, :, 1, 1:2], LN_EPS, None, ALU.add
                                ).then_inc(s[which + "var_ready"], 1)
                dve.wait_ge(s[which + "rs_ready"], n + 1)
                for j in range(2):
                    v.tensor_scalar(dst[:, j, :], src(j), bst[:, j, 1, 0:1], bst[:, j, 1, 2:3],
                                    ALU.subtract, ALU.mult).then_inc(s[ready], 1)

            def query(f, c):
                dve.wait_ge(s["q_done"], f + 1)
                v.tensor_tensor(qc[:], front_bank[:].rearrange("p (a n) -> p a n", a=2),
                                bq[:].unsqueeze(1).to_broadcast([P, 2, D]), ALU.add).then_inc(s["qc_ready"], 1)
                dve.wait_ge(s["qc_ready"], f + 1)
                for j in range(2):
                    q2 = qc[:, j, :].rearrange("p (h n two) -> p h n two", two=2, n=HD // 2)
                    o2 = qr[:, j, :].rearrange("p (h n two) -> p h n two", two=2, n=HD // 2)
                    sw = sinw[:, bass.ds(2 * f + j, 1), :].rearrange("p a (n two) -> p a n two", two=2)
                    for two in range(2):
                        c(v.tensor_tensor(o2[:, :, :, two], q2[:, :, :, 1 - two],
                                          sw[:, :, :, two].to_broadcast([P, HEADS, HD // 2]), ALU.mult))
                dve.wait_ge(s["qsq_done"], f + 1)
                c(v.tensor_reduce(qrs[:], qs[:].rearrange("p a (h d) -> p (a h) d", d=HD), AX.X, ALU.add))
                c.sync()
                v.tensor_scalar(qrs[:], qrs[:], 1.0 / HD, HEAD_EPS, ALU.mult, ALU.add).then_inc(s["qvar_ready"], 1)
                for j in range(2):
                    q3 = qc[:, j, :].rearrange("p (h d) -> p h d", d=HD)
                    c(v.tensor_tensor(q3, q3, cosw[:, bass.ds(2 * f + j, 1), :].to_broadcast([P, HEADS, HD]),
                                      ALU.mult))
                c.sync()
                c(v.tensor_tensor(qr[:], qr[:], qc[:], ALU.add))
                c.sync()
                dve.wait_ge(s["qrs_ready"], f + 1)
                q3 = qr[:].rearrange("p a (h d) -> p (a h) d", d=HD)
                c(v.tensor_tensor(q3, q3, qrs[:].unsqueeze(2).to_broadcast(q3.shape), ALU.mult))
                c.sync()
                for j in range(2):
                    q3 = qr[:, j, :].rearrange("p (h d) -> p h d", d=HD)
                    v.tensor_tensor(q3, q3, ropeb[:, bass.ds(2 * f + j, 1), :].to_broadcast([P, HEADS, HD]),
                                    ALU.add).then_inc(s["qr_ready"], 1)

            def maxima(f, j):
                for n in range(4):
                    dve.wait_ge(s["s_done"], 8 * f + 4 * j + n + 1)
                    v.tensor_reduce(mx[:, j, 4 * n:4 * n + 4],
                                    max_banks[n % 2][:, 0:4 * KEYS].rearrange("p (h n) -> p h n", n=KEYS),
                                    AX.X, ALU.max).then_inc(s["max_done"], 1)

            def split_max(f, c):
                dve.wait_ge(s["max_done"], 8 * f + 8)
                c(v.tensor_copy(m2[:, :, 0, :], mx[:]))
                c.sync()
                v.tensor_tensor(m2[:, :, 1, :], mx[:], m2[:, :, 0, :], ALU.subtract).then_inc(s["m2_ready"], 1)

            def output(t, c):
                dve.wait_ge(s["pv_done"], 8 * t + 8)
                for j in range(2):
                    o3 = pv_banks[j][:, 0:HEADS * (HD + 1)].rearrange("p (h d) -> p h d", d=HD + 1)
                    c(v.reciprocal(rden[:, j, :].unsqueeze(2), o3[:, :, HD:HD + 1]))
                c.sync()
                for j in range(2):
                    o3 = pv_banks[j][:, 0:HEADS * (HD + 1)].rearrange("p (h d) -> p h d", d=HD + 1)
                    v.tensor_tensor(on[:, j, :].rearrange("p (h d) -> p h d", d=HD), o3[:, :, 0:HD],
                                    rden[:, j, :].unsqueeze(2).to_broadcast([P, HEADS, HD]), ALU.mult
                                    ).then_inc(s["o_ready"], 1)

            def residual(t, c):
                dve.wait_ge(s["a_done"], t + 1)
                xs = xall[:, bass.ds(2 * t, 2), :]
                c(v.tensor_tensor(xs, xs, bo[:].unsqueeze(1).to_broadcast([P, 2, D]), ALU.add))
                c.sync()
                for j in range(2):
                    xj = xall[:, bass.ds(2 * t + j, 1), :].rearrange("p a d -> p (a d)")
                    v.tensor_tensor(xj, xj, tail_bank[:, j * D:(j + 1) * D], ALU.add).then_inc(s["x1_ready"], 1)
                dve.wait_ge(s["x1_ready"], 2 * t + 2)
                dve.wait_ge(s["xn2_stored"], 16 * t + 16)
                settled(dve)
                normalise(c, t, lambda j: xall[:, bass.ds(2 * t + j, 1), :].rearrange("p a d -> p (a d)"),
                          xn2, "x1", "xn2_ready")

            def logits_of():
                return max_banks[0][:, 0:2 * EXPERTS].rearrange("p (a e) -> p a e", a=2)

            def spread(ap):
                return ap.unsqueeze(2).to_broadcast([P, 2, EXPERTS])

            def each(n):
                return expert[:, n:n + 1, :].to_broadcast([P, 2, EXPERTS])

            def top2(t, c):
                dve.wait_ge(s["logits_done"], t + 1)
                c(v.tensor_reduce(gs[:, 0, :], logits_of(), AX.X, ALU.max))
                c.sync()
                v.tensor_tensor(lsub[:], logits_of(), spread(gs[:, 0, :]), ALU.subtract
                                ).then_inc(s["lsub_ready"], 1)
                dve.wait_ge(s["gexp_done"], t + 1)
                for k in range(2):
                    src = (pg, pg2)[k]
                    c(v.tensor_reduce(top[:, :, k], src[:], AX.X, ALU.max))
                    c.sync()
                    c(v.tensor_tensor(same[:], src[:], spread(top[:, :, k]), ALU.is_equal))
                    c.sync()
                    c(v.scalar_tensor_tensor(out=cand[:], in0=same[:], scalar=-float(EXPERTS), in1=each(0),
                                             op0=ALU.mult, op1=ALU.add))
                    c.sync()
                    c(v.tensor_reduce(first[:, :, k], cand[:], AX.X, ALU.min))
                    c.sync()
                    c(v.tensor_tensor(onehot[:, :, k, :], each(1), spread(first[:, :, k]), ALU.is_equal))
                    c.sync()
                    if k == 0:
                        c(v.scalar_tensor_tensor(out=pg2[:], in0=onehot[:, :, 0, :], scalar=-2.0, in1=pg[:],
                                                 op0=ALU.mult, op1=ALU.add))
                        c.sync()
                c(v.tensor_copy(cum[:, 0, :], cum[:, 2, :]))
                c(v.tensor_tensor(mask[:], onehot[:, :, 0, :], onehot[:, :, 1, :], ALU.add))
                c.sync()
                c(v.tensor_tensor(cum[:, 1, :], cum[:, 0, :], mask[:, 0, :], ALU.add))
                c.sync()
                v.tensor_tensor(cum[:, 2, :], cum[:, 1, :], mask[:, 1, :], ALU.add).then_inc(s["mask_ready"], 1)
                c(v.tensor_reduce(gs[:, 1, :], top[:], AX.X, ALU.add))
                c.sync()
                c(v.reciprocal(gs[:, 2, :], gs[:, 1, :]))
                c.sync()

            def slot_entries(t, c):
                dve.wait_ge(s["rank_done"], t + 1)
                dve.wait_ge(s["entries_written"], t + 1)
                c(v.tensor_tensor(pos[:], max_banks[1][:, 0:2 * EXPERTS].rearrange("p (a e) -> p a e", a=2),
                                  each(2), ALU.add))
                c(v.tensor_tensor(entry[:].bitcast(F32)[:, :, :, 1], top[:],
                                  gs[:, 2, :].unsqueeze(2).to_broadcast([P, 2, 2]), ALU.mult))
                c(v.tensor_copy(entry[:, :, :, 0],
                                tokens[:, bass.ds(2 * t, 2)].unsqueeze(2).to_broadcast([P, 2, 2])))
                c.sync()
                c(v.tensor_tensor(posk[:], onehot[:], pos[:].unsqueeze(2).to_broadcast([P, 2, 2, EXPERTS]), ALU.mult))
                c.sync()
                with nc.allow_low_precision(reason="a sum of one whole number and zeros"):
                    v.tensor_reduce(slots[:], posk[:], AX.X, ALU.add).then_inc(s["slots_ready"], 1)

            def step(i, b, front=False, back=False, tail=False, route=False):
                f, t = i + 1, i - 1
                r = i - 2
                cf = Steps(dve, s["front_steps"], FRONT_STEPS * f)
                ct = Steps(dve, s["tail_steps"], TAIL_STEPS * t)
                cr = Steps(dve, s["route_steps"], ROUTE_STEPS * r)
                if front:
                    normalise(cf, f, lambda j: xall[:, bass.ds(2 * f + j, 1), :].rearrange("p a d -> p (a d)"),
                              xn, "x", "xn_ready")
                if tail:
                    output(t, ct)
                if route:
                    top2(r, cr)
                if front:
                    query(f, cf)
                if route:
                    slot_entries(r, cr)
                    assert cr.n == ROUTE_STEPS, cr.n
                if tail:
                    residual(t, ct)
                    assert ct.n == TAIL_STEPS, ct.n
                if front:
                    maxima(f, 0)
                    maxima(f, 1)
                    split_max(f, cf)
                    assert cf.n == FRONT_STEPS, cf.n
            dve.wait_ge(s["x_first"], 16)
            dve.wait_ge(s["x_rest"], 16)
            dve.wait_ge(s["wo_in"], 16 * 9)
            dve.wait_ge(s["xn2_stored"], 16)
            dve.wait_ge(s["acc_stored"], 16)
            steps(dve, step)

            dve.wait_ge(s["mask_ready"], PAIRS)
            v.tensor_copy(nblk[:, 0, 0:1], nblk[:, 0, 0:1]) if False else None
            v.memset(gs[:, 3, :], 0.0).then_inc(s["cum_ready"], 1)
            dve.wait_ge(s["count_done"], 1)
            m = Steps(dve, s["meta_steps"], prep_steps)
            m(v.tensor_scalar(nblki[:, 0, :], tail_bank[0:1, 128:128 + EXPERTS], float(P - 1), None, ALU.add))
            m.sync()
            m(v.tensor_scalar(nblki[:, 1, :], nblki[:, 0, :], P.bit_length() - 1, None, ALU.arith_shift_right))
            m.sync()
            m(v.tensor_copy(nblk[:, 0, :], nblki[:, 1, :]))
            m(v.memset(metaf[:, 2, :], 1.0))
            m.sync()
            m(v.tensor_tensor_scan(nblk[:, 1, :], metaf[:, 2, 0:EXPERTS], nblk[:, 0, :], 0.0, ALU.mult, ALU.add))
            m.sync()
            wide = [1, BLOCKS, EXPERTS - 1]
            ends = nblk[:, 1:2, 0:EXPERTS - 1].to_broadcast(wide)
            m(v.tensor_tensor(ge, blockid[:].unsqueeze(2).to_broadcast(wide), ends, ALU.is_ge))
            m.sync()
            m(v.tensor_tensor(gep, ge, ends, ALU.mult))
            m(v.tensor_reduce(metaf[:, 0, :], ge, AX.X, ALU.add))
            m.sync()
            m(v.tensor_reduce(metaf[:, 1, :], gep, AX.X, ALU.max))
            m(v.tensor_copy(meta[:, 0, :], metaf[:, 0, :]))
            m.sync()
            m(v.tensor_tensor(metaf[:, 2, :], blockid[:], metaf[:, 1, :], ALU.subtract))
            m.sync()
            m(v.tensor_scalar(metaf[:, 1, :], metaf[:, 0, :], float(TOKENS // P), None, ALU.mult))
            m.sync()
            m(v.tensor_tensor(metaf[:, 2, :], metaf[:, 2, :], metaf[:, 1, :], ALU.add))
            m.sync()
            v.tensor_scalar(meta[:, 1, :], metaf[:, 2, :], float(P), None, ALU.mult).then_inc(s["meta_ready"], 1)

            def turned(n):
                dve.wait_ge(s["xgT_done"], n + 1)
                v.tensor_copy(xgTs.rearrange("p k n -> p (k n)"), xg_bank[:, 0:D]).then_inc(s["xgTs_ready"], 1)

            def expert_of(n):
                return dve.value_load(meta[0:1, 0, bass.ds(n, 1)], min_val=0, max_val=EXPERTS - 1)

            def bias(n, e):
                for a in range(2):
                    dve.wait_ge(s["hT_done"], 2 * n + a + 1)
                    v.tensor_tensor(hbT[:, 4 * a:4 * a + 4, :], hT_banks[a][:].rearrange("p (j n) -> p j n", n=P),
                                    b1s[:, bass.ds(KF * e + 4 * a, 4)].unsqueeze(2).to_broadcast([P, 4, P]),
                                    ALU.add).then_inc(s["hbT_ready"], 1)

            def result(n, e):
                c = Steps(dve, s["block_steps"], BLOCK_STEPS * n)
                dve.wait_ge(s["y_done"], n + 1)
                c(v.tensor_tensor(yb, y_bank[:, 0:D], b2s[:, bass.ds(e, 1), :].rearrange("p a d -> p (a d)"),
                                  ALU.add))
                if not (isinstance(n, int) and n == 0):
                    dve.wait_ge(s["added"], 16 * n)
                c(v.tensor_copy(sidx[:], table[:, bass.ds(n, 1), 0]))
                c.sync()
                c(v.tensor_scalar(ys, yb, table[:].bitcast(F32)[:, bass.ds(n, 1), 1], None, ALU.mult))
                c.sync()
                v.memset(gs[:, 3, :], 0.0).then_inc(s["y_ready"], 1)
                dve.wait_ge(s["y_ready"], n + 1)
                assert c.n == BLOCK_STEPS

            dve.wait_ge(s["meta_ready"], 1)
            dve.wait_ge(s["w1_in"], 16 * (EXPERTS + 1))
            dve.wait_ge(s["b2_in"], 16)
            dve.wait_ge(s["acc_stored"], 16 + 16 * PAIRS)
            turned(0)
            turned(1)
            e = expert_of(0)
            bias(0, e)
            turned(2)
            result(0, e)
            with dve.Fori(1, BLOCKS - 2) as n:
                e = expert_of(n)
                bias(n, e)
                turned(n + 2)
                result(n, e)
            for n in range(BLOCKS - 2, BLOCKS):
                e = expert_of(n)
                bias(n, e)
                result(n, e)


def kernel(x, ctx_1024, L0_xattn_q_w, L0_xattn_q_b, L0_xattn_kv_w, L0_xattn_kv_b, L0_xattn_qn_w,
           L0_xattn_qn_b, L0_xattn_kn_w, L0_xattn_kn_b, L0_xattn_out_w, L0_xattn_out_b,
           L0_ffn_gate_w, L0_ffn_w1, L0_ffn_b1, L0_ffn_w2, L0_ffn_b2):
    import numpy as np
    import ml_dtypes
    import concourse.bacc as bacc
    from concourse.bass_utils import run_bass_kernel_spmd

    bf16 = ml_dtypes.bfloat16
    place, half = np.arange(SEQ, dtype=np.float32), np.arange(0, HD, 2, dtype=np.float32)
    angle = place[:, None] * (np.float32(1.0) / np.float32(10000.0) ** (half / np.float32(HD)))[None, :]
    scale = np.float32(HD ** -0.5)
    cos = np.repeat(np.cos(angle) * scale, 2, axis=1)
    sin = np.repeat(np.sin(angle) * scale, 2, axis=1)
    sin[:, 0::2] *= -1
    sel = np.zeros((2 * HEADS, HEADS, KEYS), bf16)
    for h in range(HEADS):
        sel[h, h, :] = sel[HEADS + h, h, :] = -1
    before = np.zeros((P, 2, P), bf16)
    before[:, 0, :] = np.triu(np.ones((P, P)), 1)
    before[:, 1, :] = 1
    slots = np.zeros((SLOTS, 2), np.int32)
    slots[:, 0] = TOKENS + np.arange(SLOTS) % P
    ids = np.arange(EXPERTS, dtype=np.float32)
    expert = np.broadcast_to(np.stack([ids, ids - EXPERTS, ids * TOKENS]), (P, 3, EXPERTS))

    arrays = [x, ctx_1024, np.transpose(L0_xattn_q_w), L0_xattn_q_b, np.transpose(L0_xattn_kv_w),
              L0_xattn_kv_b, L0_xattn_qn_w, L0_xattn_qn_b, L0_xattn_kn_w, L0_xattn_kn_b,
              np.transpose(L0_xattn_out_w), L0_xattn_out_b, L0_ffn_gate_w, L0_ffn_w1, L0_ffn_b1,
              L0_ffn_w2, L0_ffn_b2,
              np.eye(P, dtype=np.float32), np.eye(P).astype(bf16), before,
              np.tile(cos, (BATCH, 1)).astype(np.float32), np.tile(sin, (BATCH, 1)).astype(np.float32),
              sel, slots, np.arange(TOKENS, dtype=np.int32).reshape(TILES, P).T, expert,
              np.arange(BLOCKS, dtype=np.float32).reshape(1, BLOCKS)]
    nc = bacc.Bacc("TRN2", target_bir_lowering=False, num_devices=1)
    given, args = {}, []
    for n, a in enumerate(arrays):
        a = np.ascontiguousarray(a)
        given[f"in_{n}"] = a
        args.append(nc.dram_tensor(f"in_{n}", a.shape, mybir.dt.from_np(a.dtype), kind="ExternalInput").ap())
    args.append(nc.dram_tensor("out_0", (BATCH, SEQ, D), F32, kind="ExternalOutput").ap())
    xattn_moe_kernel(nc, *args)
    done = run_bass_kernel_spmd(nc, [given], core_ids=[0])
    return done.results[0]["out_0"]
```

```python
from contextlib import ExitStack

import concourse.bass as bass
from concourse import mybir

F32 = mybir.dt.float32
BF16 = mybir.dt.bfloat16
I32 = mybir.dt.int32
ALU = mybir.AluOpType
ACT = mybir.ActivationFunctionType
AX = mybir.AxisListType

P = 128
BATCH, SEQ, D = 2, 1024, 256
KEYS = 77
HEADS, HD = 16, 16
EXPERTS, FF = 8, 1024
KEY_TURNS = [(b, lo, hi) for b in range(BATCH) for lo, hi in ((0, 6), (6, 12), (12, HEADS))]
TOKENS = BATCH * SEQ
TILES = TOKENS // P
PAIRS = TILES // 2
PAIRS_B = PAIRS // BATCH
KD = D // P
KF = FF // P
HPC = HEADS // KD
BLOCKS = 2 * TOKENS // P + EXPERTS - 1
SLOTS = (EXPERTS - 1) * TOKENS + BLOCKS * P
ROWS = TOKENS + P
LN_EPS, HEAD_EPS = 1e-5, 1e-6
FRONT_STEPS = 27
NORM_STEPS = 4
OUTPUT_STEPS = 2
TAIL_STEPS = 4
ROUTE_STEPS = 18
BLOCK_STEPS = 2
W1_RING = 3


class Steps:

    def __init__(self, eng, sem, base=0):
        self.eng, self.sem, self.base, self.n = eng, sem, base, 0

    def __call__(self, ins):
        ins.then_inc(self.sem, 1)
        self.n += 1

    def sync(self):
        self.eng.wait_ge(self.sem, self.base + self.n)


def xattn_moe_kernel(nc, x, ctx_in, wqT, q_b, wkvT, kv_b, qn_w, qn_b, kn_w, kn_b, woT, out_b,
                     gate_w, w1, b1, w2, b2, c_ident, c_identb, c_upper, c_cos, c_sin, c_sel,
                     c_slots, c_tokens, c_expert, c_block, out):
    x_v = x.rearrange("b (t p) d -> p (b t) d", p=P)
    out_rows = out.rearrange("b s d -> (b s) d")
    slot_table = nc.dram_tensor("slot_table", (SLOTS, 2), I32).ap()
    xn2_rows = nc.dram_tensor("xn2_rows", (ROWS, D), F32).ap()
    acc_rows = nc.dram_tensor("acc_rows", (ROWS, D), F32).ap()

    with ExitStack() as ctx:
        def sb(name, shape, dt=F32):
            return ctx.enter_context(nc.sbuf_tensor(name, shape, dt))

        def sem(name):
            return ctx.enter_context(nc.semaphore(name))

        banks = [ctx.enter_context(nc.psum_tensor(f"bank{n}", [P, 512], F32)) for n in range(8)]
        front_bank, tail_bank = banks[0], banks[1]
        cT_banks, kv_banks = banks[6:8], banks[2:4]
        key_banks = banks[4:8] + [banks[1], banks[2]]
        max_banks, score_banks, pv_banks = banks[2:4], banks[4:6], banks[6:8]
        max_ring = max_banks + score_banks
        hT_banks, y_bank, xg_bank = banks[6:8], banks[2], banks[0]

        ident, identb = sb("ident", [P, P]), sb("identb", [P, P], BF16)
        upper = sb("upper", [P, 2, P], BF16)
        sel = sb("sel", [2 * HEADS, HEADS, KEYS], BF16)
        cosw, sinw, ropeb = (sb(n, [P, TILES, HD]) for n in ("cosw", "sinw", "ropeb"))
        hw = sb("hw", [P, 4, HD])
        hws = sb("hws", [P, 2, HD])
        tokens = sb("tokens", [P, TILES], I32)
        expert = sb("expert", [P, 2 + 2 * EXPERTS, EXPERTS])
        blockid = sb("blockid", [1, BLOCKS])
        wq, wo = sb("wq", [P, KD, D]), sb("wo", [P, KD, D])
        bq, bo = sb("bq", [P, D]), sb("bo", [P, D])
        gw = sb("gw", [P, KD, EXPERTS])
        w1b = sb("w1b", [P, W1_RING, KD, FF])
        w2s = sb("w2s", [P, EXPERTS * KF, D])
        b1s = sb("b1s", [P, EXPERTS * KF])
        wsum = sb("wsum", [P, 2 * KD * HEADS + 2 * HEADS])

        kzT = [sb(f"kzT{b}", [P, HEADS, KEYS]) for b in range(BATCH)]
        vaug = [sb(f"vaug{b}", [KEYS, HEADS, HD + 1]) for b in range(BATCH)]
        xall = sb("xall", [P, TILES, D])
        probs = sb("probs", [P, HEADS, 2 * P])
        ctx_temp = [probs, sb("ctx_temp1", [P, 12, 2 * P])]
        kz_flat = [temp[0:KEYS, 0:9, :].rearrange("p h n -> p (h n)") for temp in ctx_temp]
        kc = [temp[0:KEYS, 9, :] for temp in ctx_temp]
        cT = [temp[:, 10, 0:KD * KEYS].rearrange("p (k n) -> p k n", k=KD) for temp in ctx_temp]
        cin = [temp[0:KEYS, 11, :] for temp in ctx_temp]
        ksq = cin
        krs = sb("krs", [KEYS, BATCH, HEADS])
        cosb = sb("cosb", [P, TILES, HD])
        power = sb("power", [P, 1])
        wkv = probs[:, 12:16, :].rearrange("p (k a) n -> p k (a n)", k=KD)
        bst, bst2 = sb("bst", [P, 2, 2, 8]), sb("bst2", [P, 2, 2, 8])
        xn = sb("xn", [P, 2, D])
        xnTs = sb("xnTs", [P, 2, KD, P])
        qc = sb("qc", [P, 2, D])
        qs = sb("qs", [P, 2, D])
        bkv = qc[0:KEYS, :, :].rearrange("p a n -> p (a n)")
        qrs = sb("qrs", [P, 2 * HEADS])
        root = sb("root", [P, 2, 2 * HEADS])
        kroot = sb("kroot", [KEYS, 2, BATCH * HEADS])
        qr = xn
        qTs = sb("qTs", [P, KD, 2 * P])
        mx = sb("mx", [P, 2, HEADS])
        m2 = sb("m2", [P, 2, 2, HEADS], BF16)
        mTs = sb("mTs", [2 * HEADS, 2 * P], BF16)
        rden = sb("rden", [P, 2, HEADS])
        on = sb("on", [P, 2, D])
        oTs = sb("oTs", [P, 2, KD, P])
        xn2 = sb("xn2", [P, 2, D])
        xn2Ts = sb("xn2Ts", [P, 2, KD, P])
        lsub, pg = sb("lsub", [P, 2, EXPERTS]), sb("pg", [P, 2, EXPERTS])
        ahead_of = sb("ahead_of", [P, 2, EXPERTS, 2 * EXPERTS])[:]
        rank = sb("rank", [P, 2, EXPERTS])
        gs = sb("gs", [P, 4, 2])
        top = sb("top", [P, 2, 2])
        onehot = sb("onehot", [P, 2, 2, EXPERTS])
        mask = sb("mask", [P, 2, EXPERTS], BF16)
        cum = sb("cum", [P, 3, EXPERTS], BF16)
        pos = sb("pos", [P, 2, EXPERTS])
        posk = sb("posk", [P, 2, 2, EXPERTS])
        slots = sb("slots", [P, 2, 2], I32)
        entry = sb("entry", [P, 2, 2, 2], I32)
        nblk, nblki = sb("nblk", [1, 2, EXPERTS]), sb("nblki", [1, 2, EXPERTS], I32)
        ge, gep = (buf[0:1, :, :].rearrange("p a n -> p (a n)")[:, 0:BLOCKS * (EXPERTS - 1)]
                   .rearrange("p (b e) -> p b e", b=BLOCKS) for buf in (qc, qs))
        metaf = (xn[0:1, :, :].rearrange("p a n -> p (a n)")[:, 0:3 * BLOCKS]
                 .rearrange("p (a n) -> p a n", a=3))
        meta = qTs[0:1, 1, 0:2 * BLOCKS].bitcast(I32).rearrange("p (a n) -> p a n", a=2)
        table = qTs[:, 0, 0:2 * BLOCKS].bitcast(I32).rearrange("p (n c) -> p n c", c=2)
        gidx, sidx = sb("gidx", [P, 1], I32), sb("sidx", [P, 1], I32)
        b2s = sb("b2s", [P, EXPERTS, D])
        hTs = probs[:, 8:12, :].rearrange("p a (b n) -> p (a b) n", n=P)
        xg, yb, ys = probs[:, 12, :], probs[:, 13, :], probs[:, 14, :]
        xgTs = probs[:, 15, :].rearrange("p (k n) -> p k n", n=P)
        hbT = xall[:, 4:8, :].rearrange("p t (a n) -> p (t a) n", n=P)

        names = """const_in rope_in wq_in wkv_in wo_in hw_in ctx_in x_first x_rest b1_in w2_in b2_in paced
            power_ready xvar_ready xrs_ready x1var_ready x1rs_ready rope_steps rope_ready prep
            cT_done cTs_ready kv_done kc_ready ksq_done kz_ready kzT_done kzT_ready vaug_ready
            front_steps output_steps tail_steps route_steps xn_ready xT_done xnTs_ready q_done qc_ready
            qsq_done qr_ready qT_done qTs_ready s_done max_done m2_ready mT_done mTs_ready
            st_done exp_done pv_done o_ready oT_done oTs_ready a_done x1_ready xn2_ready xn2_stored
            acc_stored xn2T_done xn2Ts_ready logits_done lsub_ready gexp_done mask_ready rank_done
            slots_ready padded scattered entries_written cum_ready count_done meta_steps meta_ready
            table_in idx_ready gathered xgT_done xgTs_ready hT_done hbT_ready
            gelu_done y_done yb_ready block_steps y_ready added out_stored""".split()
        s = {n: sem(n) for n in names}
        w1_in = [sem(f"w1_in{n}") for n in range(W1_RING)]

        def settled(eng):
            eng.sem_inc(s["paced"], 1)

        def steps(eng, step):
            step(-1, 0, front=True, ahead=True)
            step(0, 0, front=True, back=True, ahead=True)
            step(1, 0, front=True, back=True, tail=True, ahead=True)
            with eng.Fori(2, PAIRS_B) as i:
                step(i, 0, front=True, back=True, tail=True, route=True, ahead=True)
            with eng.Fori(PAIRS_B, PAIRS - 2) as i:
                step(i, 1, front=True, back=True, tail=True, route=True, ahead=True)
            step(PAIRS - 2, 1, front=True, back=True, tail=True, route=True)
            step(PAIRS - 1, 1, back=True, tail=True, route=True)
            step(PAIRS, 1, tail=True, route=True)
            step(PAIRS + 1, 1, route=True)

        w1_v = w1.rearrange("e (k p) f -> p (e k) f", p=P)
        block = ctx.enter_context(nc.Block())

        @block.sync
        def _(sp):
            sp.dma_start(cin[0], ctx_in[0]).then_inc(s["ctx_in"], 16)
            sp.dma_start(cin[1], ctx_in[1]).then_inc(s["ctx_in"], 16)
            sp.dma_start(wkv, wkvT.rearrange("(k p) n -> p k n", p=P)).then_inc(s["wkv_in"], 16)
            sp.dma_start(ident[:], c_ident).then_inc(s["const_in"], 16)
            sp.dma_start(bkv, kv_b.partition_broadcast(KEYS)).then_inc(s["const_in"], 16)
            sp.dma_start(xall[:, 0:2, :], x_v[:, 0:2, :]).then_inc(s["x_first"], 16)
            sp.dma_start(wq[:], wqT.rearrange("(k p) n -> p k n", p=P)).then_inc(s["wq_in"], 16)
            sp.dma_start(bq[:], q_b.partition_broadcast(P)).then_inc(s["wq_in"], 16)
            for n, v in enumerate((qn_w, qn_b, kn_w, kn_b)):
                sp.dma_start(hw[:, n, :], v.partition_broadcast(P)).then_inc(s["hw_in"], 16)
            sp.dma_start(cosw[:], c_cos.rearrange("(t p) n -> p t n", p=P)).then_inc(s["rope_in"], 16)
            sp.dma_start(sinw[:], c_sin.rearrange("(t p) n -> p t n", p=P)).then_inc(s["rope_in"], 16)
            sp.dma_start(identb[:], c_identb).then_inc(s["wo_in"], 16)
            sp.dma_start(sel[:], c_sel).then_inc(s["wo_in"], 16)
            sp.dma_start(xall[:, 2:TILES, :], x_v[:, 2:TILES, :]).then_inc(s["x_rest"], 16)
            sp.dma_start(wo[:], woT.rearrange("(k p) n -> p k n", p=P)).then_inc(s["wo_in"], 16)
            sp.dma_start(bo[:], out_b.partition_broadcast(P)).then_inc(s["wo_in"], 16)
            sp.dma_start(gw[:], gate_w.rearrange("(k p) n -> p k n", p=P)).then_inc(s["wo_in"], 16)
            sp.dma_start(upper[:], c_upper).then_inc(s["wo_in"], 16)
            sp.dma_start(tokens[:], c_tokens).then_inc(s["wo_in"], 16)
            sp.dma_start(expert[:], c_expert).then_inc(s["wo_in"], 16)
            sp.dma_start(blockid[:], c_block).then_inc(s["wo_in"], 16)
            sp.dma_start(slot_table, c_slots).then_inc(s["padded"], 16)
            sp.wait_ge(s["prep"], 1)
            sp.dma_start(xn2_rows[TOKENS:ROWS, :], on[:, 0, :]).then_inc(s["xn2_stored"], 16)
            sp.dma_start(acc_rows[TOKENS:ROWS, :], on[:, 0, :]).then_inc(s["acc_stored"], 16)
            sp.dma_start(b1s[:], b1.rearrange("e (j p) -> p (e j)", p=P),
                         allow_slow_non_contiguous=True).then_inc(s["b1_in"], 16)
            for e in range(EXPERTS):
                sp.dma_start(w2s[:, KF * e:KF * e + KF, :], w2[e].rearrange("(j p) d -> p j d", p=P)
                             ).then_inc(s["w2_in"], 16)
            sp.dma_start(b2s[:], b2.partition_broadcast(P)).then_inc(s["b2_in"], 16)

            def step(i, b, front=False, back=False, tail=False, route=False, ahead=False):
                t = i - 1
                if tail:
                    sp.wait_ge(s["x1_ready"], 2 * t + 2)
                    sp.dma_start(
                        acc_rows[0:TOKENS, :].rearrange("(t p) d -> p t d", p=P)[:, bass.ds(2 * t, 2), :],
                        xall[:, bass.ds(2 * t, 2), :]).then_inc(s["acc_stored"], 16)
                    sp.wait_ge(s["xn2_ready"], 2 * t + 2)
                    sp.dma_start(
                        xn2_rows[0:TOKENS, :].rearrange("(t p) d -> p t d", p=P)[:, bass.ds(2 * t, 2), :],
                        xn2[:]).then_inc(s["xn2_stored"], 16)

            steps(sp, step)
            def w1_load(n, place):
                e = sp.value_load(meta[0:1, 0, bass.ds(n, 1)], min_val=0, max_val=EXPERTS - 1)
                sp.dma_start(w1b[:, place, :, :], w1_v[:, bass.ds(KD * e, KD), :]).then_inc(w1_in[place], 16)

            def table_load(n):
                start = sp.value_load(meta[0:1, 1, bass.ds(n, 1)], min_val=0, max_val=SLOTS - P)
                sp.dma_start(table[:, bass.ds(n, 1), :],
                             slot_table[bass.ds(start, P), :].rearrange("p (a c) -> p a c", a=1)
                             ).then_inc(s["table_in"], 16)
                sp.wait_ge(s["table_in"], 16 * n + 16)
                settled(sp)

            sp.wait_ge(s["meta_ready"], 1)
            w1_load(0, 0)
            sp.wait_ge(s["entries_written"], 1 + PAIRS)
            table_load(0)
            table_load(1)
            sp.wait_ge(s["gathered"], 16)
            w1_load(1, 1)
            for n in range(2, W1_RING):
                table_load(n)
                w1_load(n, n)
            with sp.Fori(0, BLOCKS // W1_RING - 1) as m:
                for place in range(W1_RING):
                    n = W1_RING * m + place
                    table_load(n + W1_RING)
                    sp.wait_ge(s["hT_done"], 2 * n + 2)
                    settled(sp)
                    w1_load(n + W1_RING, place)
            sp.wait_ge(s["added"], 16 * BLOCKS)
            sp.dma_start(out_rows.rearrange("(a r) d -> a (r d)", a=P),
                         acc_rows[0:TOKENS, :].rearrange("(a r) d -> a (r d)", a=P)
                         ).then_inc(s["out_stored"], 16)
            sp.wait_ge(s["out_stored"], 16)

        @block.gpsimd
        def _(pool):
            def power_of(which, n, buf):
                pool.wait_ge(s[which + "var_ready"], n + 1)
                nc.gpsimd.tensor_tensor(buf, buf, power[0:buf.shape[0], :].to_broadcast(buf.shape), ALU.pow
                                        ).then_inc(s[which + "rs_ready"], 1)

            def step(i, tail=False, route=False, ahead=False):
                t, r = i - 1, i - 2
                if ahead:
                    power_of("x", i + 2, bst[:, :, 1, 2])
                if tail:
                    power_of("x1", t, bst2[:, :, 1, 2])
                if route:
                    pool.wait_ge(s["slots_ready"], r + 1)
                    settled(pool)
                    for j in range(2):
                        for k in range(2):
                            nc.gpsimd.indirect_dma_start(
                                slot_table, bass.IndirectOffsetOnAxis(ap=slots[:, j, k:k + 1], axis=0),
                                entry[:, j, k, :], None).then_inc(s["scattered"], 16)
                    pool.wait_ge(s["scattered"], 64 * r + 64)
                    pool.sem_inc(s["entries_written"], 1)

            nc.gpsimd.memset(power[:], -0.5).then_inc(s["power_ready"], 1)
            pool.wait_ge(s["power_ready"], 1)
            power_of("x", 0, bst[:, :, 1, 2])
            c = Steps(pool, s["rope_steps"])
            pool.wait_ge(s["hw_in"], 64)
            for n in range(2):
                two = hw[:, n, :].rearrange("p (n two) -> p n two", two=2)
                c(nc.gpsimd.tensor_copy(hws[:, n, :].rearrange("p (n two) -> p n two", two=2), two[:, :, ::-1]))
            c.sync()
            pool.wait_ge(s["rope_in"], 32)
            tab = [P, TILES, HD]

            def times(out, table, scale):
                return nc.gpsimd.tensor_tensor(out[:], table[:], scale.to_broadcast(tab), ALU.mult)

            c(times(ropeb, sinw, hws[:, 1:2, :]))
            c(times(cosb, cosw, hw[:, 1:2, :]))
            c.sync()
            c(times(sinw, sinw, hws[:, 0:1, :]))
            c(nc.gpsimd.tensor_tensor(ropeb[:], ropeb[:], cosb[:], ALU.add))
            times(cosw, cosw, hw[:, 0:1, :]).then_inc(s["rope_ready"], 1)
            c.sync()
            pool.sem_inc(s["rope_ready"], 1)
            pool.wait_ge(s["padded"], 16)
            pool.sem_inc(s["entries_written"], 1)
            step(-1, ahead=True)
            step(0, ahead=True)
            step(1, tail=True, ahead=True)
            with pool.Fori(2, PAIRS - 2) as i:
                step(i, tail=True, route=True, ahead=True)
            step(PAIRS - 2, tail=True, route=True)
            step(PAIRS - 1, tail=True, route=True)
            step(PAIRS, tail=True, route=True)
            step(PAIRS + 1, route=True)

            def gather(n):
                pool.wait_ge(s["table_in"], 16 * n + 16)
                settled(pool)
                nc.gpsimd.tensor_copy(gidx[:], table[:, bass.ds(n, 1), 0]).then_inc(s["idx_ready"], 1)
                pool.wait_ge(s["idx_ready"], n + 1)
                settled(pool)
                nc.gpsimd.indirect_dma_start(
                    xg, None, xn2_rows, bass.IndirectOffsetOnAxis(ap=gidx[:, 0:1], axis=0)
                ).then_inc(s["gathered"], 16)

            def add_back(n):
                settled(pool)
                nc.gpsimd.indirect_dma_start(
                    acc_rows, bass.IndirectOffsetOnAxis(ap=sidx[:, 0:1], axis=0), ys, None,
                    compute_op=ALU.add).then_inc(s["added"], 16)

            pool.wait_ge(s["xn2_stored"], 16 + 16 * PAIRS)
            pool.wait_ge(s["acc_stored"], 16 + 16 * PAIRS)
            gather(0)
            for n in range(1, 3):
                pool.wait_ge(s["xgT_done"], n)
                gather(n)
            with pool.Fori(0, BLOCKS - 3) as n:
                pool.wait_ge(s["xgT_done"], n + 3)
                gather(n + 3)
                pool.wait_ge(s["y_ready"], n + 1)
                add_back(n)
            for n in range(BLOCKS - 3, BLOCKS):
                pool.wait_ge(s["y_ready"], n + 1)
                add_back(n)

        @block.scalar
        def _(act):
            def bank_to(buf, bank):
                return nc.scalar.copy(buf[:].rearrange("p a b n -> p (a b n)"), bank[:])

            def rows_turned(f):
                act.wait_ge(s["xT_done"], f + 1)
                bank_to(xnTs, front_bank).then_inc(s["xnTs_ready"], 1)

            def squares(f):
                act.wait_ge(s["qc_ready"], f + 1)
                nc.scalar.activation(qs[:], qc[:], ACT.Square).then_inc(s["qsq_done"], 1)

            def rows2_turned(r, bank):
                act.wait_ge(s["xn2T_done"], r + 1)
                bank_to(xn2Ts, bank).then_inc(s["xn2Ts_ready"], 1)

            for b in range(BATCH):
                act.wait_ge(s["cT_done"], b + 1)
                nc.scalar.copy(cT[b], cT_banks[b][:, 0:KD * KEYS].rearrange("p (k n) -> p k n", k=KD)
                               ).then_inc(s["cTs_ready"], 1)
            for b in range(BATCH):
                act.wait_ge(s["kc_ready"], b + 1)
                nc.scalar.activation(ksq[b], kc[b], ACT.Square).then_inc(s["ksq_done"], 1)
            rows_turned(0)
            squares(0)
            for n, (b, lo, hi) in enumerate(KEY_TURNS):
                act.wait_ge(s["kzT_done"], n + 1)
                nc.scalar.copy(kzT[b][:, lo:hi, :],
                               key_banks[n][:, 0:(hi - lo) * KEYS].rearrange("p (h n) -> p h n", n=KEYS)
                               ).then_inc(s["kzT_ready"], 1)
            def exp(i, g):
                act.wait_ge(s["st_done"], 8 * i + g + 1)
                nc.scalar.activation(probs[0:KEYS, 2 * g:2 * g + 2, :],
                                     score_banks[g % 2][0:KEYS, :].rearrange("p (a n) -> p a n", a=2),
                                     ACT.Exp).then_inc(s["exp_done"], 1)

            def step(i, b, front=False, back=False, tail=False, route=False, ahead=False):
                f, t, r = i + 1, i - 1, i - 2
                if back:
                    exp(i, 0)
                    exp(i, 1)
                if front and back:
                    rows_turned(f)
                if back:
                    exp(i, 2)
                if route and not back:
                    rows2_turned(r, front_bank)
                if tail:
                    act.wait_ge(s["oT_done"], t + 1)
                    bank_to(oTs, tail_bank).then_inc(s["oTs_ready"], 1)
                if route and back:
                    rows2_turned(r, tail_bank if front else front_bank)
                if front and back:
                    squares(f)
                if back:
                    exp(i, 3)
                if route:
                    act.wait_ge(s["lsub_ready"], r + 1)
                    nc.scalar.activation(pg[:], lsub[:], ACT.Exp).then_inc(s["gexp_done"], 1)
                if back:
                    for g in range(4, 8):
                        exp(i, g)
                if front:
                    act.wait_ge(s["qT_done"], f + 1)
                    nc.scalar.copy(qTs[:].rearrange("p c n -> p (c n)"), front_bank[:]
                                   ).then_inc(s["qTs_ready"], 1)
                    act.wait_ge(s["mT_done"], f + 1)
                    nc.scalar.copy(mTs[:], front_bank[0:2 * HEADS, 0:P].bitcast(BF16)
                                   ).then_inc(s["mTs_ready"], 1)
            steps(act, step)

            def gelu(n):
                for a in range(2):
                    act.wait_ge(s["hbT_ready"], 2 * n + a + 1)
                    nc.scalar.activation(hTs[:, 4 * a:4 * a + 4, :], hbT[:, 4 * a:4 * a + 4, :],
                                         ACT.Gelu).then_inc(s["gelu_done"], 1)

            gelu(0)
            with act.Fori(1, BLOCKS) as n:
                act.wait_ge(s["y_done"], n)
                gelu(n)

        @block.tensor
        def _(pe):
            mm = nc.tensor.matmul

            pe.wait_ge(s["ctx_in"], 32)
            pe.wait_ge(s["const_in"], 32)
            for b in range(BATCH):
                for k in range(KD):
                    last = nc.tensor.transpose(cT_banks[b][:, k * KEYS:(k + 1) * KEYS],
                                               cin[b][:, k * P:(k + 1) * P], ident[0:KEYS, 0:KEYS])
                last.then_inc(s["cT_done"], 1)
            pe.wait_ge(s["prep"], 2)
            for b in range(BATCH):
                pe.wait_ge(s["cTs_ready"], b + 1)
                for k in range(KD):
                    last = mm(kv_banks[b][0:KEYS, :], cT[b][:, k, :], wkv[:, k, :], start=k == 0, stop=k == KD - 1)
                last.then_inc(s["kv_done"], 1)

            def scores(i, b, g):
                if g == 0:
                    pe.wait_ge(s["mTs_ready"], i + 1)
                if not (isinstance(i, int) and i == 0 and g < 2):
                    pe.wait_ge(s["exp_done"], 8 * i + g - 1)
                for a in range(2):
                    h = 2 * g + a
                    to = score_banks[g % 2][0:KEYS, a * 2 * P:(a + 1) * 2 * P]
                    mm(to, kzT[b][:, h, :], qTs[:, h // HPC, :], start=True, stop=False)
                    last = mm(to, sel[:, h, :], mTs[:], start=False, stop=True)
                last.then_inc(s["st_done"], 1)

            def values(i, b, g):
                pe.wait_ge(s["exp_done"], 8 * i + g + 1)
                if g == 0 and not (isinstance(i, int) and i == 0):
                    pe.wait_ge(s["o_ready"], 2 * i)
                for j in range(2):
                    for h in (2 * g, 2 * g + 1):
                        last = mm(pv_banks[j][:, h * (HD + 1):(h + 1) * (HD + 1)],
                                  probs[0:KEYS, h, j * P:(j + 1) * P], vaug[b][:, h, :],
                                  start=True, stop=True)
                last.then_inc(s["pv_done"], 1)

            def maxima(f, j):
                n = 0
                if j == 0:
                    pe.wait_ge(s["qTs_ready"], f + 1)
                kb = kz_of(f)
                for c in range(KD):
                    for g in range(2):
                        if not (isinstance(f, int) and f == 0 and j == 0 and n < 4):
                            pe.wait_ge(s["max_done"], 8 * f + 4 * j + n - 3)
                        mm(max_ring[n][:, 0:4 * KEYS], qTs[:, c, j * P:(j + 1) * P],
                           kb[:, HPC * c + 4 * g:HPC * c + 4 * g + 4, :].rearrange("p h n -> p (h n)"),
                           start=True, stop=True).then_inc(s["s_done"], 1)
                        n += 1

            front_batch = [0]

            def kz_of(f):
                return kzT[front_batch[0]]

            def transposes(bank, src, split):
                for j in range(2):
                    for k in range(KD):
                        at = (2 * j + k if split else 2 * k + j) * P
                        last = nc.tensor.transpose(bank[:, at:at + P], src[:, j, k * P:(k + 1) * P], ident[:])
                return last

            def rows2_turn(r, bank):
                pe.wait_ge(s["xn2_ready"], 2 * r + 2)
                transposes(bank, xn2, True).then_inc(s["xn2T_done"], 1)

            def project(bank, lhs, w, n):
                for j in range(2):
                    for k in range(KD):
                        last = mm(bank[:, j * n:(j + 1) * n], lhs[:, j, k, :], w[:, k, :],
                                  start=k == 0, stop=k == KD - 1)
                return last

            def step(i, b, front=False, back=False, tail=False, route=False, ahead=False):
                f, t, r = i + 1, i - 1, i - 2
                if back:
                    scores(i, b, 0)
                    scores(i, b, 1)
                if front and back:
                    pe.wait_ge(s["xn_ready"], 2 * f + 2)
                    pe.wait_ge(s["mTs_ready"], f)
                    transposes(front_bank, xn, True).then_inc(s["xT_done"], 1)
                if back:
                    scores(i, b, 2)
                if route and not back:
                    rows2_turn(r, front_bank)
                    pe.wait_ge(s["xn2Ts_ready"], r + 1)
                    project(max_banks[0], xn2Ts, gw, EXPERTS).then_inc(s["logits_done"], 1)
                if tail:
                    pe.wait_ge(s["o_ready"], 2 * t + 2)
                    if not (isinstance(t, int) and t == 0):
                        pe.wait_ge(s["x1_ready"], 2 * t)
                    transposes(tail_bank, on, True).then_inc(s["oT_done"], 1)
                if front and back:
                    pe.wait_ge(s["xnTs_ready"], f + 1)
                    project(front_bank, xnTs, wq, D).then_inc(s["q_done"], 1)
                if tail:
                    pe.wait_ge(s["oTs_ready"], t + 1)
                if route and back:
                    rows2_turn(r, tail_bank if front else front_bank)
                if tail and not front:
                    project(tail_bank, oTs, wo, D).then_inc(s["a_done"], 1)
                if back:
                    scores(i, b, 3)
                if route and back:
                    pe.wait_ge(s["xn2Ts_ready"], r + 1)
                    project(max_banks[0], xn2Ts, gw, EXPERTS).then_inc(s["logits_done"], 1)
                if tail and front:
                    project(tail_bank, oTs, wo, D).then_inc(s["a_done"], 1)
                if back:
                    values(i, b, 0)
                    scores(i, b, 4)
                    scores(i, b, 5)
                    values(i, b, 1)
                    scores(i, b, 6)
                if route:
                    pe.wait_ge(s["mask_ready"], r + 1)
                    for j in range(2):
                        to = max_banks[1][:, j * EXPERTS:(j + 1) * EXPERTS]
                        mm(to, upper[:, 0, :], mask[:, j, :], start=True, stop=False)
                        last = mm(to, upper[:, 1, :], cum[:, j, :], start=False, stop=True)
                    last.then_inc(s["rank_done"], 1)
                if back:
                    values(i, b, 2)
                    scores(i, b, 7)
                    values(i, b, 3)
                if front:
                    pe.wait_ge(s["qr_ready"], 2 * f + 2)
                    transposes(front_bank, qr, False).then_inc(s["qT_done"], 1)
                if back:
                    values(i, b, 4)
                if front:
                    if route:
                        pe.wait_ge(s["slots_ready"], r + 1)
                    if back:
                        pe.wait_ge(s["exp_done"], 8 * i + 8)
                    maxima(f, 0)
                if back:
                    values(i, b, 5)
                if front:
                    maxima(f, 1)
                if back:
                    values(i, b, 6)
                if front:
                    pe.wait_ge(s["m2_ready"], f + 1)
                    for j in range(2):
                        last = nc.tensor.transpose(
                            front_bank[0:2 * HEADS, j * P // 2:(j + 1) * P // 2].bitcast(BF16),
                            m2[:, j, :, :].rearrange("p a h -> p (a h)"), identb[:])
                    last.then_inc(s["mT_done"], 1)
                if back:
                    values(i, b, 7)
            pe.wait_ge(s["xn_ready"], 2)
            transposes(front_bank, xn, True).then_inc(s["xT_done"], 1)
            pe.wait_ge(s["prep"], 3)
            pe.wait_ge(s["xnTs_ready"], 1)
            project(front_bank, xnTs, wq, D).then_inc(s["q_done"], 1)
            pe.wait_ge(s["kz_ready"], 1)
            pe.wait_ge(s["vaug_ready"], BATCH)
            for n, (b, lo, hi) in enumerate(KEY_TURNS):
                for h in range(lo, hi):
                    last = nc.tensor.transpose(key_banks[n][:, (h - lo) * KEYS:(h - lo + 1) * KEYS],
                                               kz_flat[b][:, h * P:(h + 1) * P], ident[0:KEYS, 0:KEYS])
                last.then_inc(s["kzT_done"], 1)
            pe.wait_ge(s["kzT_ready"], len(KEY_TURNS))
            pe.wait_ge(s["wo_in"], 16 * 9)
            step(-1, 0, front=True)
            step(0, 0, front=True, back=True)
            step(1, 0, front=True, back=True, tail=True)
            step(2, 0, front=True, back=True, tail=True, route=True)
            front_batch[0] = 1
            step(3, 0, front=True, back=True, tail=True, route=True)
            with pe.Fori(PAIRS_B, PAIRS - 1) as i:
                step(i, 1, front=True, back=True, tail=True, route=True)
            step(PAIRS - 1, 1, back=True, tail=True, route=True)
            step(PAIRS, 1, tail=True, route=True)
            step(PAIRS + 1, 1, route=True)
            pe.wait_ge(s["cum_ready"], 1)
            mm(tail_bank[:, 128:128 + EXPERTS], upper[:, 1, :], cum[:, 2, :], start=True, stop=True
               ).then_inc(s["count_done"], 1)

            def xg_turn(n):
                pe.wait_ge(s["gathered"], 16 * n + 16)
                for k in range(KD):
                    last = nc.tensor.transpose(xg_bank[:, k * P:(k + 1) * P], xg[:, k * P:(k + 1) * P], ident[:])
                last.then_inc(s["xgT_done"], 1)

            def expert_of(n):
                return pe.value_load(meta[0:1, 0, bass.ds(n, 1)], min_val=0, max_val=EXPERTS - 1)

            def up(n, m, place):
                pe.wait_ge(w1_in[place], 16 * m + 16)
                pe.wait_ge(s["xgTs_ready"], n + 1)
                for j in range(KF):
                    if j % 4 == 0 and not (isinstance(n, int) and n == 0):
                        pe.wait_ge(s["hbT_ready"], 2 * n + j // 4 - 1)
                    for k in range(KD):
                        last = mm(hT_banks[j // 4][:, (j % 4) * P:(j % 4 + 1) * P],
                                  w1b[:, place, k, j * P:(j + 1) * P], xgTs[:, k, :],
                                  start=k == 0, stop=k == KD - 1)
                    if j % 4 == 3:
                        last.then_inc(s["hT_done"], 1)

            def down(n, e):
                if not (isinstance(n, int) and n == 0):
                    pe.wait_ge(s["yb_ready"], n)
                for j in range(KF):
                    if j % 4 == 0:
                        pe.wait_ge(s["gelu_done"], 2 * n + j // 4 + 1)
                    last = mm(y_bank[:, 0:D], hTs[:, j, :],
                              w2s[:, bass.ds(KF * e + j, 1), :].rearrange("p a d -> p (a d)"),
                              start=j == 0, stop=j == KF - 1)
                last.then_inc(s["y_done"], 1)

            pe.wait_ge(s["meta_ready"], 1)
            pe.wait_ge(s["w2_in"], 16 * EXPERTS)
            xg_turn(0)
            up(0, 0, 0)
            pe.wait_ge(s["xgTs_ready"], 1)
            xg_turn(1)
            def blocks(m):
                for j in range(W1_RING):
                    n = W1_RING * m + j
                    e = expert_of(n)
                    up(n + 1, m + (j + 1) // W1_RING, (j + 1) % W1_RING)
                    xg_turn(n + 2)
                    down(n, e)

            blocks(0)
            with pe.Fori(1, BLOCKS // W1_RING - 1) as m:
                blocks(m)
            for n in range(BLOCKS - W1_RING, BLOCKS):
                e = expert_of(n)
                if n + 1 < BLOCKS:
                    up(n + 1, (n + 1) // W1_RING, (n + 1) % W1_RING)
                if n + 2 < BLOCKS:
                    xg_turn(n + 2)
                down(n, e)

        @block.vector
        def _(dve):
            v = nc.vector
            prep = Steps(dve, s["meta_steps"])

            def centre(w, sums):
                w3 = w.rearrange("p (h d) -> p h d", d=HD)
                prep(v.tensor_reduce(sums, w3, AX.X, ALU.add))
                prep.sync()
                return v.scalar_tensor_tensor(
                    out=w3, in0=sums.unsqueeze(2).to_broadcast(w3.shape), scalar=-1.0 / HD,
                    in1=w3, op0=ALU.mult, op1=ALU.add)

            def normalise(c, n, src, dst, bst, which, ready, meanwhile=None):
                for j in range(2):
                    c(v.bn_stats(bst[:, j, 0, 0:6], src(j)))
                c.sync()
                settled(dve)
                for j in range(2):
                    c(v.bn_aggr(bst[:, j, 1, 0:2], bst[:, j, 0, 0:6]))
                c.sync()
                v.tensor_scalar(bst[:, :, 1, 2:3], bst[:, :, 1, 1:2], LN_EPS, None, ALU.add
                                ).then_inc(s[which + "var_ready"], 1)
                if meanwhile:
                    meanwhile()
                dve.wait_ge(s[which + "rs_ready"], n + 1)
                for j in range(2):
                    v.tensor_scalar(dst[:, j, :], src(j), bst[:, j, 1, 0:1], bst[:, j, 1, 2:3],
                                    ALU.subtract, ALU.mult).then_inc(s[ready], 1)

            def norm_front(c, f, meanwhile=None):
                normalise(c, f, lambda j: xall[:, bass.ds(2 * f + j, 1), :].rearrange("p a d -> p (a d)"),
                          xn, bst, "x", "xn_ready", meanwhile)

            def query(f, c, routing):
                dve.wait_ge(s["q_done"], f + 1)
                v.tensor_tensor(qc[:], front_bank[:].rearrange("p (a n) -> p a n", a=2),
                                bq[:].unsqueeze(1).to_broadcast([P, 2, D]), ALU.add).then_inc(s["qc_ready"], 1)
                dve.wait_ge(s["qc_ready"], f + 1)
                for j in range(2):
                    q2 = qc[:, j, :].rearrange("p (h n two) -> p h n two", two=2, n=HD // 2)
                    o2 = qr[:, j, :].rearrange("p (h n two) -> p h n two", two=2, n=HD // 2)
                    sw = sinw[:, bass.ds(2 * f + j, 1), :].rearrange("p a (n two) -> p a n two", two=2)
                    for two in range(2):
                        c(v.tensor_tensor(o2[:, :, :, two], q2[:, :, :, 1 - two],
                                          sw[:, :, :, two].to_broadcast([P, HEADS, HD // 2]), ALU.mult))
                dve.wait_ge(s["qsq_done"], f + 1)
                c(v.tensor_reduce(qrs[:], qs[:].rearrange("p a (h d) -> p (a h) d", d=HD), AX.X, ALU.add))
                c.sync()
                c(v.tensor_scalar(qrs[:], qrs[:], 1.0 / HD, HEAD_EPS, ALU.mult, ALU.add))
                for j in range(2):
                    q3 = qc[:, j, :].rearrange("p (h d) -> p h d", d=HD)
                    c(v.tensor_tensor(q3, q3, cosw[:, bass.ds(2 * f + j, 1), :].to_broadcast([P, HEADS, HD]),
                                      ALU.mult))
                routing(0)
                c.sync()
                y, h = root[:, 0, :], root[:, 1, :]
                c(v.tensor_scalar(h.bitcast(I32), qrs[:].bitcast(I32), 1, None, ALU.arith_shift_right))
                routing(1)
                c.sync()
                c(v.tensor_scalar(y.bitcast(I32), h.bitcast(I32), -1.0, float(0x5F3759DF), ALU.mult, ALU.add))
                c(v.tensor_tensor(qr[:], qr[:], qc[:], ALU.add))
                routing(2)
                c.sync()
                for n in range(3):
                    c(v.tensor_tensor(h, y, y, ALU.mult))
                    routing(3 * n + 3)
                    c.sync()
                    c(v.scalar_tensor_tensor(out=h, in0=h, scalar=-0.5, in1=qrs[:], op0=ALU.mult, op1=ALU.mult))
                    routing(3 * n + 4)
                    c.sync()
                    c(v.scalar_tensor_tensor(out=y, in0=h, scalar=1.5, in1=y, op0=ALU.add, op1=ALU.mult))
                    routing(3 * n + 5)
                    c.sync()
                q3 = qr[:].rearrange("p a (h d) -> p (a h) d", d=HD)
                c(v.tensor_tensor(q3, q3, y.unsqueeze(2).to_broadcast(q3.shape), ALU.mult))
                c.sync()
                for j in range(2):
                    q3 = qr[:, j, :].rearrange("p (h d) -> p h d", d=HD)
                    v.tensor_tensor(q3, q3, ropeb[:, bass.ds(2 * f + j, 1), :].to_broadcast([P, HEADS, HD]),
                                    ALU.add).then_inc(s["qr_ready"], 1)

            def maxima(f, j):
                for n in range(4):
                    dve.wait_ge(s["s_done"], 8 * f + 4 * j + n + 1)
                    v.tensor_reduce(mx[:, j, 4 * n:4 * n + 4],
                                    max_ring[n][:, 0:4 * KEYS].rearrange("p (h n) -> p h n", n=KEYS),
                                    AX.X, ALU.max).then_inc(s["max_done"], 1)

            def split_max(f, c):
                dve.wait_ge(s["max_done"], 8 * f + 8)
                c(v.tensor_copy(m2[:, :, 0, :], mx[:]))
                c.sync()
                v.tensor_tensor(m2[:, :, 1, :], mx[:], m2[:, :, 0, :], ALU.subtract).then_inc(s["m2_ready"], 1)

            def output(t, c):
                if isinstance(t, int) and t == 0:
                    dve.wait_ge(s["xn2_stored"], 16)
                    dve.wait_ge(s["acc_stored"], 16)
                dve.wait_ge(s["pv_done"], 8 * t + 8)
                for j in range(2):
                    o3 = pv_banks[j][:, 0:HEADS * (HD + 1)].rearrange("p (h d) -> p h d", d=HD + 1)
                    c(v.reciprocal(rden[:, j, :].unsqueeze(2), o3[:, :, HD:HD + 1]))
                c.sync()
                for j in range(2):
                    o3 = pv_banks[j][:, 0:HEADS * (HD + 1)].rearrange("p (h d) -> p h d", d=HD + 1)
                    v.tensor_tensor(on[:, j, :].rearrange("p (h d) -> p h d", d=HD), o3[:, :, 0:HD],
                                    rden[:, j, :].unsqueeze(2).to_broadcast([P, HEADS, HD]), ALU.mult
                                    ).then_inc(s["o_ready"], 1)

            def residual(t, c):
                dve.wait_ge(s["a_done"], t + 1)
                for j in range(2):
                    xj = xall[:, bass.ds(2 * t + j, 1), :].rearrange("p a d -> p (a d)")
                    v.tensor_tensor(xj, xj, tail_bank[:, j * D:(j + 1) * D], ALU.add).then_inc(s["x1_ready"], 1)
                dve.wait_ge(s["x1_ready"], 2 * t + 2)
                dve.wait_ge(s["xn2_stored"], 16 * t + 16)
                if not (isinstance(t, int) and t == 0):
                    dve.wait_ge(s["xn2T_done"], t)
                settled(dve)
                normalise(c, t, lambda j: xall[:, bass.ds(2 * t + j, 1), :].rearrange("p a d -> p (a d)"),
                          xn2, bst2, "x1", "xn2_ready")

            def logits_of():
                return max_banks[0][:, 0:2 * EXPERTS].rearrange("p (a e) -> p a e", a=2)

            def spread(ap):
                return ap.unsqueeze(2).to_broadcast([P, 2, EXPERTS])

            def route_part(t, c, n):
                if n == 0:
                    dve.wait_ge(s["logits_done"], t + 1)
                    c(v.tensor_reduce(gs[:, 0, :], logits_of(), AX.X, ALU.max))
                elif n == 1:
                    c.sync()
                    v.tensor_tensor(lsub[:], logits_of(), spread(gs[:, 0, :]), ALU.subtract
                                    ).then_inc(s["lsub_ready"], 1)
                elif n == 2:
                    dve.wait_ge(s["lsub_ready"], t + 1)
                    pairs = [P, 2, EXPERTS, EXPERTS]
                    for k, op in enumerate((ALU.is_ge, ALU.is_gt)):
                        c(v.tensor_tensor(ahead_of[:, :, :, k * EXPERTS:(k + 1) * EXPERTS],
                                          lsub[:].unsqueeze(2).to_broadcast(pairs),
                                          lsub[:].unsqueeze(3).to_broadcast(pairs), op))
                elif n == 3:
                    c.sync()
                    flat = ahead_of.rearrange("p a e n -> p a (e n)")
                    order = expert[:, 2:2 + 2 * EXPERTS, :].rearrange("p a e -> p (a e)")
                    c(v.tensor_tensor(flat, flat, order.unsqueeze(1).to_broadcast([P, 2, 2 * EXPERTS * EXPERTS]),
                                      ALU.mult))
                elif n == 4:
                    c.sync()
                    c(v.tensor_reduce(rank[:], ahead_of, AX.X, ALU.add))
                elif n == 5:
                    c.sync()
                    for k in range(2):
                        c(v.tensor_scalar(onehot[:, :, k, :], rank[:], float(k), None, ALU.is_equal))
                    c(v.tensor_copy(cum[:, 0, :], cum[:, 2, :]))
                elif n == 6:
                    c.sync()
                    c(v.tensor_tensor(mask[:], onehot[:, :, 0, :], onehot[:, :, 1, :], ALU.add))
                elif n == 7:
                    c.sync()
                    c(v.tensor_tensor(cum[:, 1, :], cum[:, 0, :], mask[:, 0, :], ALU.add))
                elif n == 8:
                    c.sync()
                    v.tensor_tensor(cum[:, 2, :], cum[:, 1, :], mask[:, 1, :], ALU.add
                                    ).then_inc(s["mask_ready"], 1)
                elif n == 9:
                    dve.wait_ge(s["gexp_done"], t + 1)
                    c(v.tensor_tensor(posk[:], onehot[:], pg[:].unsqueeze(2).to_broadcast([P, 2, 2, EXPERTS]),
                                      ALU.mult))
                elif n == 10:
                    c.sync()
                    c(v.tensor_reduce(top[:], posk[:], AX.X, ALU.add))
                elif n == 11:
                    c.sync()
                    c(v.tensor_reduce(gs[:, 1, :], top[:], AX.X, ALU.add))

            def slot_entries(t, c):
                c.sync()
                c(v.reciprocal(gs[:, 2, :], gs[:, 1, :]))
                c.sync()
                dve.wait_ge(s["rank_done"], t + 1)
                dve.wait_ge(s["entries_written"], t + 1)
                c(v.tensor_tensor(pos[:], max_banks[1][:, 0:2 * EXPERTS].rearrange("p (a e) -> p a e", a=2),
                                  expert[:, 1:2, :].to_broadcast([P, 2, EXPERTS]), ALU.add))
                c(v.tensor_tensor(entry[:].bitcast(F32)[:, :, :, 1], top[:],
                                  gs[:, 2, :].unsqueeze(2).to_broadcast([P, 2, 2]), ALU.mult))
                c(v.tensor_copy(entry[:, :, :, 0],
                                tokens[:, bass.ds(2 * t, 2)].unsqueeze(2).to_broadcast([P, 2, 2])))
                c.sync()
                c(v.tensor_tensor(posk[:], onehot[:], pos[:].unsqueeze(2).to_broadcast([P, 2, 2, EXPERTS]), ALU.mult))
                c.sync()
                with nc.allow_low_precision(reason="a sum of one whole number and zeros"):
                    v.tensor_reduce(slots[:], posk[:], AX.X, ALU.add).then_inc(s["slots_ready"], 1)

            def step(i, b, front=False, back=False, tail=False, route=False, ahead=False):
                f, t = i + 1, i - 1
                r = i - 2
                cf = Steps(dve, s["front_steps"], NORM_STEPS + FRONT_STEPS * f)
                co = Steps(dve, s["output_steps"], OUTPUT_STEPS * i)
                ct = Steps(dve, s["tail_steps"], TAIL_STEPS * t)
                cr = Steps(dve, s["route_steps"], ROUTE_STEPS * r)
                first = front and not back

                def routing(n):
                    if route:
                        route_part(r, cr, n)
                    elif first:
                        key_part(n)

                if front:
                    query(f, cf, routing)
                else:
                    for n in range(12):
                        routing(n)
                if route:
                    slot_entries(r, cr)
                    assert cr.n == ROUTE_STEPS, cr.n
                if front:
                    if first:
                        dve.wait_ge(s["x_rest"], 16)
                        dve.wait_ge(s["wo_in"], 16 * 9)
                    xs = xall[:, bass.ds(2 * f, 2), :]
                    cf(v.tensor_tensor(xs, xs, bo[:].unsqueeze(1).to_broadcast([P, 2, D]), ALU.add))
                    maxima(f, 0)
                    maxima(f, 1)
                    split_max(f, cf)
                if ahead:
                    norm_front(cf, f + 1, (lambda: output(i, co)) if back else None)
                    assert cf.n == FRONT_STEPS, cf.n
                if tail:
                    residual(t, ct)
                    assert ct.n == TAIL_STEPS, ct.n
                if back and not ahead:
                    output(i, co)

            v.memset(on[:, 0, :], 0.0).then_inc(s["prep"], 1)
            for b in range(BATCH):
                prep(v.memset(kz_flat[b][:, 0:HEADS * P], 0.0))
                prep(v.memset(vaug[b][:], 1.0))
            prep(v.memset(cum[:], 0.0))
            dve.wait_ge(s["wkv_in"], 16)
            prep(centre(wkv[:, 0, 0:D], wsum[:, 0:16]))
            centre(wkv[:, 1, 0:D], wsum[:, 32:48]).then_inc(s["prep"], 1)
            dve.wait_ge(s["const_in"], 32)
            prep(centre(bkv[:, 0:D], wsum[0:KEYS, 16:32]))
            dve.wait_ge(s["x_first"], 16)
            norm_front(Steps(dve, s["front_steps"]), 0)
            dve.wait_ge(s["wq_in"], 32)
            prep(centre(wq[:, 0, :], wsum[:, 48:64]))
            prep(centre(bq[:], wsum[:, 64:80]))
            centre(wq[:, 1, :], wsum[:, 80:96]).then_inc(s["prep"], 1)
            prep.sync()

            for b in range(BATCH):
                dve.wait_ge(s["kv_done"], b + 1)
                v.tensor_tensor(kc[b], kv_banks[b][0:KEYS, 0:D], bkv[:, 0:D], ALU.add).then_inc(s["kc_ready"], 1)
            for b in range(BATCH):
                v.tensor_tensor(vaug[b][:, :, 0:HD],
                                kv_banks[b][0:KEYS, D:2 * D].rearrange("p (h d) -> p h d", d=HD),
                                bkv[:, D:2 * D].rearrange("p (h d) -> p h d", d=HD), ALU.add
                                ).then_inc(s["vaug_ready"], 1)
            for b in range(BATCH):
                dve.wait_ge(s["ksq_done"], b + 1)
                prep(v.tensor_reduce(krs[:, b, :], ksq[b].rearrange("p (h d) -> p h d", d=HD), AX.X, ALU.add))
            prep.sync()
            kvar = krs[:].rearrange("p b h -> p (b h)")
            prep(v.tensor_scalar(kvar, kvar, 1.0 / HD, HEAD_EPS, ALU.mult, ALU.add))
            prep.sync()
            y, h = kroot[:, 0, :], kroot[:, 1, :]
            prep(v.tensor_scalar(h.bitcast(I32), kvar.bitcast(I32), 1, None, ALU.arith_shift_right))
            prep.sync()
            prep(v.tensor_scalar(y.bitcast(I32), h.bitcast(I32), -1.0, float(0x5F3759DF), ALU.mult, ALU.add))
            dve.wait_ge(s["hw_in"], 64)
            k3 = [kc[b].rearrange("p (h d) -> p h d", d=HD) for b in range(BATCH)]

            def key_part(n):
                prep.sync()
                if n < 9 and n % 3 == 0:
                    prep(v.tensor_tensor(h, y, y, ALU.mult))
                elif n < 9 and n % 3 == 1:
                    prep(v.scalar_tensor_tensor(out=h, in0=h, scalar=-0.5, in1=kvar, op0=ALU.mult, op1=ALU.mult))
                elif n < 9:
                    prep(v.scalar_tensor_tensor(out=y, in0=h, scalar=1.5, in1=y, op0=ALU.add, op1=ALU.mult))
                elif n == 9:
                    for b in range(BATCH):
                        prep(v.tensor_tensor(k3[b], k3[b], y[:, HEADS * b:HEADS * (b + 1)].unsqueeze(2)
                                             .to_broadcast(k3[b].shape), ALU.mult))
                elif n == 10:
                    for b in range(BATCH):
                        prep(v.tensor_tensor(k3[b], k3[b], hw[0:KEYS, 2:3, :].to_broadcast(k3[b].shape), ALU.mult))
                else:
                    for b in range(BATCH):
                        for c in range(KD):
                            to = (kz_flat[b][:, HPC * P * c:HPC * P * c + HPC * (P + HD)]
                                  .rearrange("p (h n) -> p h n", n=P + HD)[:, :, 0:HD])
                            from3 = k3[b][:, HPC * c:HPC * (c + 1), :]
                            prep(v.tensor_tensor(to, from3, hw[0:KEYS, 3:4, :].to_broadcast(from3.shape), ALU.add))
                    prep.sync()
                    v.memset(gs[:, 3, :], 0.0).then_inc(s["kz_ready"], 1)


            dve.wait_ge(s["rope_ready"], 2)
            steps(dve, step)

            dve.wait_ge(s["mask_ready"], PAIRS)
            v.memset(gs[:, 3, :], 0.0).then_inc(s["cum_ready"], 1)
            dve.wait_ge(s["count_done"], 1)
            m = Steps(dve, s["meta_steps"], prep.n)
            m(v.tensor_scalar(nblki[:, 0, :], tail_bank[0:1, 128:128 + EXPERTS], float(P - 1), None, ALU.add))
            m.sync()
            m(v.tensor_scalar(nblki[:, 1, :], nblki[:, 0, :], P.bit_length() - 1, None, ALU.arith_shift_right))
            m.sync()
            m(v.tensor_copy(nblk[:, 0, :], nblki[:, 1, :]))
            m(v.memset(metaf[:, 2, :], 1.0))
            m.sync()
            m(v.tensor_tensor_scan(nblk[:, 1, :], metaf[:, 2, 0:EXPERTS], nblk[:, 0, :], 0.0, ALU.mult, ALU.add))
            m.sync()
            wide = [1, BLOCKS, EXPERTS - 1]
            ends = nblk[:, 1:2, 0:EXPERTS - 1].to_broadcast(wide)
            m(v.tensor_tensor(ge, blockid[:].unsqueeze(2).to_broadcast(wide), ends, ALU.is_ge))
            m.sync()
            m(v.tensor_tensor(gep, ge, ends, ALU.mult))
            m(v.tensor_reduce(metaf[:, 0, :], ge, AX.X, ALU.add))
            m.sync()
            m(v.tensor_reduce(metaf[:, 1, :], gep, AX.X, ALU.max))
            m(v.tensor_copy(meta[:, 0, :], metaf[:, 0, :]))
            m.sync()
            m(v.tensor_tensor(metaf[:, 2, :], blockid[:], metaf[:, 1, :], ALU.subtract))
            m.sync()
            m(v.tensor_scalar(metaf[:, 1, :], metaf[:, 0, :], float(TOKENS // P), None, ALU.mult))
            m.sync()
            m(v.tensor_tensor(metaf[:, 2, :], metaf[:, 2, :], metaf[:, 1, :], ALU.add))
            m.sync()
            v.tensor_scalar(meta[:, 1, :], metaf[:, 2, :], float(P), None, ALU.mult).then_inc(s["meta_ready"], 1)

            def turned(n):
                dve.wait_ge(s["xgT_done"], n + 1)
                v.tensor_copy(xgTs.rearrange("p k n -> p (k n)"), xg_bank[:, 0:D]).then_inc(s["xgTs_ready"], 1)

            def expert_of(n):
                return dve.value_load(meta[0:1, 0, bass.ds(n, 1)], min_val=0, max_val=EXPERTS - 1)

            def bias(n, e):
                for a in range(2):
                    dve.wait_ge(s["hT_done"], 2 * n + a + 1)
                    if not (isinstance(n, int) and n == 0):
                        dve.wait_ge(s["gelu_done"], 2 * n + a - 1)
                    v.tensor_tensor(hbT[:, 4 * a:4 * a + 4, :], hT_banks[a][:].rearrange("p (j n) -> p j n", n=P),
                                    b1s[:, bass.ds(KF * e + 4 * a, 4)].unsqueeze(2).to_broadcast([P, 4, P]),
                                    ALU.add).then_inc(s["hbT_ready"], 1)

            def result(n, e):
                c = Steps(dve, s["block_steps"], BLOCK_STEPS * n)
                dve.wait_ge(s["y_done"], n + 1)
                v.tensor_tensor(yb, y_bank[:, 0:D], b2s[:, bass.ds(e, 1), :].rearrange("p a d -> p (a d)"),
                                ALU.add).then_inc(s["yb_ready"], 1)
                if not (isinstance(n, int) and n == 0):
                    dve.wait_ge(s["added"], 16 * n)
                c(v.tensor_copy(sidx[:], table[:, bass.ds(n, 1), 0]))
                dve.wait_ge(s["yb_ready"], n + 1)
                c(v.tensor_scalar(ys, yb, table.bitcast(F32)[:, bass.ds(n, 1), 1], None, ALU.mult))
                c.sync()
                v.memset(gs[:, 3, :], 0.0).then_inc(s["y_ready"], 1)
                dve.wait_ge(s["y_ready"], n + 1)
                assert c.n == BLOCK_STEPS

            dve.wait_ge(s["meta_ready"], 1)
            dve.wait_ge(s["b1_in"], 16)
            dve.wait_ge(s["b2_in"], 16)
            dve.wait_ge(s["acc_stored"], 16 + 16 * PAIRS)
            turned(0)
            bias(0, expert_of(0))
            turned(1)
            bias(1, expert_of(1))
            turned(2)
            result(0, expert_of(0))
            with dve.Fori(1, BLOCKS - 2) as n:
                bias(n + 1, expert_of(n + 1))
                turned(n + 2)
                result(n, expert_of(n))
            bias(BLOCKS - 1, expert_of(BLOCKS - 1))
            for n in range(BLOCKS - 2, BLOCKS):
                result(n, expert_of(n))


def kernel(x, ctx_1024, L0_xattn_q_w, L0_xattn_q_b, L0_xattn_kv_w, L0_xattn_kv_b, L0_xattn_qn_w,
           L0_xattn_qn_b, L0_xattn_kn_w, L0_xattn_kn_b, L0_xattn_out_w, L0_xattn_out_b,
           L0_ffn_gate_w, L0_ffn_w1, L0_ffn_b1, L0_ffn_w2, L0_ffn_b2):
    import numpy as np
    import ml_dtypes
    import concourse.bacc as bacc
    from concourse.bass_utils import run_bass_kernel_spmd

    bf16 = ml_dtypes.bfloat16
    place, half = np.arange(SEQ, dtype=np.float32), np.arange(0, HD, 2, dtype=np.float32)
    angle = place[:, None] * (np.float32(1.0) / np.float32(10000.0) ** (half / np.float32(HD)))[None, :]
    scale = np.float32(HD ** -0.5)
    cos = np.repeat(np.cos(angle) * scale, 2, axis=1)
    sin = np.repeat(np.sin(angle) * scale, 2, axis=1)
    sin[:, 0::2] *= -1
    sel = np.zeros((2 * HEADS, HEADS, KEYS), bf16)
    for h in range(HEADS):
        sel[h, h, :] = sel[HEADS + h, h, :] = -1
    before = np.zeros((P, 2, P), bf16)
    before[:, 0, :] = np.triu(np.ones((P, P)), 1)
    before[:, 1, :] = 1
    slots = np.zeros((SLOTS, 2), np.int32)
    slots[:, 0] = TOKENS + np.arange(SLOTS) % P
    ids = np.arange(EXPERTS, dtype=np.float32)
    order = np.concatenate([ids[None, :] < ids[:, None], ids[None, :] > ids[:, None]], axis=1)
    expert = np.concatenate([np.stack([ids, ids * TOKENS]),
                             order.astype(np.float32).reshape(2 * EXPERTS, EXPERTS)])
    expert = np.broadcast_to(expert, (P,) + expert.shape)

    arrays = [x, ctx_1024, np.transpose(L0_xattn_q_w), L0_xattn_q_b, np.transpose(L0_xattn_kv_w),
              L0_xattn_kv_b, L0_xattn_qn_w, L0_xattn_qn_b, L0_xattn_kn_w, L0_xattn_kn_b,
              np.transpose(L0_xattn_out_w), L0_xattn_out_b, L0_ffn_gate_w, L0_ffn_w1, L0_ffn_b1,
              L0_ffn_w2, L0_ffn_b2,
              np.eye(P, dtype=np.float32), np.eye(P).astype(bf16), before,
              np.tile(cos, (BATCH, 1)).astype(np.float32), np.tile(sin, (BATCH, 1)).astype(np.float32),
              sel, slots, np.arange(TOKENS, dtype=np.int32).reshape(TILES, P).T, expert,
              np.arange(BLOCKS, dtype=np.float32).reshape(1, BLOCKS)]
    nc = bacc.Bacc("TRN2", target_bir_lowering=False, num_devices=1)
    given, args = {}, []
    for n, a in enumerate(arrays):
        a = np.ascontiguousarray(a)
        given[f"in_{n}"] = a
        args.append(nc.dram_tensor(f"in_{n}", a.shape, mybir.dt.from_np(a.dtype), kind="ExternalInput").ap())
    args.append(nc.dram_tensor("out_0", (BATCH, SEQ, D), F32, kind="ExternalOutput").ap())
    xattn_moe_kernel(nc, *args)
    done = run_bass_kernel_spmd(nc, [given], core_ids=[0])
    return done.results[0]["out_0"]
```
